# Optimizing a Trainium2 kernel written in Bass

```python
import numpy as np
import jax
import jax.numpy as jnp

def _softmax(x, axis=-1):
    return jax.nn.softmax(x, axis=axis)

def _gelu(x):
    return jax.nn.gelu(x, approximate=True)

def _silu(x):
    return jax.nn.silu(x)

def _sigmoid(x):
    return jax.nn.sigmoid(x)

def _layernorm(x, axis=-1, eps=1e-05):
    m = jnp.mean(x, axis=axis, keepdims=True)
    v = jnp.var(x, axis=axis, keepdims=True)
    return (x - m) / jnp.sqrt(v + eps)

def _scatter_add(tgt, idx, src, axis=0):
    return tgt.at[idx].add(src)

def _segment_sum(src, seg, n):
    return jax.ops.segment_sum(src, seg, n)
kernel_name = 'mk_seq_postln_d1_jaxref_r8_62df2b'

def setup_inputs(seed: int=0):
    np.random.seed(seed)
    _w = jnp.asarray

    def _L0_attn_setup():
        import jax, jax.numpy as jnp
        import numpy as np
        NUM_BLOCKS = 4
        B, S, D = (4, 512, 128)
        A, FF = (128, 512)
        LN_EPS = 1e-06

        def _ln(x, s, b):
            m = jnp.mean(x, axis=-1, keepdims=True)
            v = jnp.mean(jnp.square(x - m), axis=-1, keepdims=True)
            return (x - m) * jax.lax.rsqrt(v + LN_EPS) * s + b
        key = jax.random.key(seed)
        ks = jax.random.split(key, 8)
        w = lambda k, shape: jax.random.normal(k, shape, dtype=jnp.float32) * 0.02
        return {'x': jax.random.normal(ks[0], (B, S, D), dtype=jnp.float32), 'Wq': w(ks[1], (NUM_BLOCKS, D, A)), 'bq': jnp.zeros((NUM_BLOCKS, A), jnp.float32), 'Wk': w(ks[2], (NUM_BLOCKS, D, A)), 'bk': jnp.zeros((NUM_BLOCKS, A), jnp.float32), 'Wv': w(ks[3], (NUM_BLOCKS, D, A)), 'bv': jnp.zeros((NUM_BLOCKS, A), jnp.float32), 'Wo': w(ks[4], (NUM_BLOCKS, A, D)), 'bo': jnp.zeros((NUM_BLOCKS, D), jnp.float32), 'ln1_s': jnp.ones((NUM_BLOCKS, D), jnp.float32), 'ln1_b': jnp.zeros((NUM_BLOCKS, D), jnp.float32), 'W1': w(ks[5], (NUM_BLOCKS, D, FF)), 'b1': jnp.zeros((NUM_BLOCKS, FF), jnp.float32), 'W2': w(ks[6], (NUM_BLOCKS, FF, D)), 'b2': jnp.zeros((NUM_BLOCKS, D), jnp.float32), 'ln2_s': jnp.ones((NUM_BLOCKS, D), jnp.float32), 'ln2_b': jnp.zeros((NUM_BLOCKS, D), jnp.float32)}
    _L0_attn_in = _L0_attn_setup()

    def _L0_ffn_setup():
        import jax, jax.numpy as jnp
        import numpy as np
        EPS = 1e-06
        LN_EPS = 1e-05

        def _absmean_core(W):
            gamma = jnp.mean(jnp.abs(W)) + EPS
            Ws = W / gamma
            Wq = jnp.sign(Ws) * jnp.minimum(jnp.round(jnp.abs(Ws)), 1.0)
            return (Wq, gamma)

        @jax.custom_vjp
        def absmean(W):
            return _absmean_core(W)[0]

        def _absmean_fwd(W):
            Wq, gamma = _absmean_core(W)
            return (Wq, gamma)

        def _absmean_bwd(gamma, g):
            return (g / gamma,)
        absmean.defvjp(_absmean_fwd, _absmean_bwd)

        def layernorm(x, w, b, eps=LN_EPS):
            mu = jnp.mean(x, axis=-1, keepdims=True)
            var = jnp.mean((x - mu) ** 2, axis=-1, keepdims=True)
            return (x - mu) * jax.lax.rsqrt(var + eps) * w + b
        key = jax.random.key(seed)
        k1, k2, k3 = jax.random.split(key, 3)
        d, h = (128, 512)
        B, T = (8, 256)
        return {'x': jax.random.normal(k1, (B, T, d), jnp.float32), 'W_fc': jax.random.normal(k2, (h, d), jnp.float32), 'ln_w': jnp.ones((h,), jnp.float32), 'ln_b': jnp.zeros((h,), jnp.float32), 'W_proj': jax.random.normal(k3, (d, h), jnp.float32)}
    _L0_ffn_in = _L0_ffn_setup()
    _d = {'L0_attn_x': _L0_attn_in['x'], 'L0_attn_Wq': _L0_attn_in['Wq'], 'L0_attn_bq': _L0_attn_in['bq'], 'L0_attn_Wk': _L0_attn_in['Wk'], 'L0_attn_bk': _L0_attn_in['bk'], 'L0_attn_Wv': _L0_attn_in['Wv'], 'L0_attn_bv': _L0_attn_in['bv'], 'L0_attn_Wo': _L0_attn_in['Wo'], 'L0_attn_bo': _L0_attn_in['bo'], 'L0_attn_ln1_s': _L0_attn_in['ln1_s'], 'L0_attn_ln1_b': _L0_attn_in['ln1_b'], 'L0_attn_W1': _L0_attn_in['W1'], 'L0_attn_b1': _L0_attn_in['b1'], 'L0_attn_W2': _L0_attn_in['W2'], 'L0_attn_b2': _L0_attn_in['b2'], 'L0_attn_ln2_s': _L0_attn_in['ln2_s'], 'L0_attn_ln2_b': _L0_attn_in['ln2_b'], 'L0_ffn_W_fc': _L0_ffn_in['W_fc'], 'L0_ffn_ln_w': _L0_ffn_in['ln_w'], 'L0_ffn_ln_b': _L0_ffn_in['ln_b'], 'L0_ffn_W_proj': _L0_ffn_in['W_proj']}
    _x0 = _d['L0_attn_x']
    _d['L0_attn_x'] = jax.random.normal(jax.random.fold_in(jax.random.key(seed), 1), (2, 2048, 128), dtype=_x0.dtype)
    del _x0
    return _d

def reference(L0_attn_x, L0_attn_Wq, L0_attn_bq, L0_attn_Wk, L0_attn_bk, L0_attn_Wv, L0_attn_bv, L0_attn_Wo, L0_attn_bo, L0_attn_ln1_s, L0_attn_ln1_b, L0_attn_W1, L0_attn_b1, L0_attn_W2, L0_attn_b2, L0_attn_ln2_s, L0_attn_ln2_b, L0_ffn_W_fc, L0_ffn_ln_w, L0_ffn_ln_b, L0_ffn_W_proj):

    def _L0_attn_ref(x, Wq, bq, Wk, bk, Wv, bv, Wo, bo, ln1_s, ln1_b, W1, b1, W2, b2, ln2_s, ln2_b):
        import jax, jax.numpy as jnp
        import numpy as np
        NUM_BLOCKS = 4
        B, S, D = (4, 512, 128)
        A, FF = (128, 512)
        LN_EPS = 1e-06

        def _ln(x, s, b):
            m = jnp.mean(x, axis=-1, keepdims=True)
            v = jnp.mean(jnp.square(x - m), axis=-1, keepdims=True)
            return (x - m) * jax.lax.rsqrt(v + LN_EPS) * s + b
        for i in range(NUM_BLOCKS):
            residual = x
            q = x @ Wq[i] + bq[i]
            k = x @ Wk[i] + bk[i]
            v = x @ Wv[i] + bv[i]
            Q = jax.nn.elu(q) + 1.0
            K = jax.nn.elu(k) + 1.0
            KV = jnp.einsum('nsh,nsh->nh', K, v, precision='highest')
            Ksum = jnp.sum(K, axis=1)
            Z = 1.0 / (Q * Ksum[:, None, :] + 1e-06)
            V = Q * KV[:, None, :] * Z
            a = jax.nn.gelu(V @ Wo[i] + bo[i])
            a = jax.nn.gelu(a)
            x = _ln(a + residual, ln1_s[i], ln1_b[i])
            residual = x
            h = jax.nn.gelu(x @ W1[i] + b1[i])
            f = jax.nn.gelu(h @ W2[i] + b2[i])
            x = _ln(f + residual, ln2_s[i], ln2_b[i])
        return x

    def _L0_ffn_ref(x, W_fc, ln_w, ln_b, W_proj):
        import jax, jax.numpy as jnp
        import numpy as np
        EPS = 1e-06
        LN_EPS = 1e-05

        def _absmean_core(W):
            gamma = jnp.mean(jnp.abs(W)) + EPS
            Ws = W / gamma
            Wq = jnp.sign(Ws) * jnp.minimum(jnp.round(jnp.abs(Ws)), 1.0)
            return (Wq, gamma)

        @jax.custom_vjp
        def absmean(W):
            return _absmean_core(W)[0]

        def _absmean_fwd(W):
            Wq, gamma = _absmean_core(W)
            return (Wq, gamma)

        def _absmean_bwd(gamma, g):
            return (g / gamma,)
        absmean.defvjp(_absmean_fwd, _absmean_bwd)

        def layernorm(x, w, b, eps=LN_EPS):
            mu = jnp.mean(x, axis=-1, keepdims=True)
            var = jnp.mean((x - mu) ** 2, axis=-1, keepdims=True)
            return (x - mu) * jax.lax.rsqrt(var + eps) * w + b
        h = jnp.einsum('btd,hd->bth', x, absmean(W_fc))
        h = jax.nn.gelu(h, approximate=False)
        h = layernorm(h, ln_w, ln_b)
        return jnp.einsum('bth,dh->btd', h, absmean(W_proj))
    x = L0_attn_x
    x = _layernorm(x + _L0_attn_ref(x, L0_attn_Wq, L0_attn_bq, L0_attn_Wk, L0_attn_bk, L0_attn_Wv, L0_attn_bv, L0_attn_Wo, L0_attn_bo, L0_attn_ln1_s, L0_attn_ln1_b, L0_attn_W1, L0_attn_b1, L0_attn_W2, L0_attn_b2, L0_attn_ln2_s, L0_attn_ln2_b), axis=-1)
    x = _layernorm(x + _L0_ffn_ref(x, L0_ffn_W_fc, L0_ffn_ln_w, L0_ffn_ln_b, L0_ffn_W_proj), axis=-1)
    return x

_drawn_inputs = setup_inputs


def setup_inputs(seed=0):
    import zlib

    import numpy as np

    out = dict(_drawn_inputs(seed))
    spreads = {'L0_attn_bq': (0.0, 2.0),
     'L0_attn_bk': (0.0, 0.8),
     'L0_attn_bv': (0.0, 0.8),
     'L0_attn_bo': (0.0, 0.1),
     'L0_attn_ln1_s': (1.0, 0.2),
     'L0_attn_ln1_b': (0.0, 0.1),
     'L0_attn_b1': (0.0, 0.523),
     'L0_attn_b2': (0.0, 0.1),
     'L0_attn_ln2_s': (1.0, 0.2),
     'L0_attn_ln2_b': (0.0, 0.1),
     'L0_ffn_ln_w': (1.0, 0.2),
     'L0_ffn_ln_b': (0.0, 0.1)}
    factors = {'L0_attn_Wq': 64.0, 'L0_attn_Wk': 8.0, 'L0_attn_Wv': 8.0, 'L0_attn_Wo': 8.0}
    for name, (base, spread) in spreads.items():
        noise = np.random.default_rng([zlib.crc32(name.encode()), seed]).standard_normal(out[name].shape)
        drawn = base * np.exp(spread * noise) if base else spread * noise
        out[name] = jnp.asarray(drawn.astype(out[name].dtype))
    for name, factor in factors.items():
        out[name] = (out[name] * factor).astype(out[name].dtype)
    return out
```

```python
from contextlib import ExitStack

import concourse.bass as bass
from concourse import mybir

P = 128
LAYERS = 4
BATCHES = 2
SEQ = 2048
TOKENS = BATCHES * SEQ
BANK = 512
PAIR = 2 * BANK
PAIRS = TOKENS // PAIR
PAIRS_PER_BATCH = PAIRS // BATCHES
FF = 512
FT = FF // P
ROW = 128
ROWS = SEQ // ROW
ROWS_PER_PAIR = PAIR // ROW
LOW = 32
ZEPS = 1e-6
BLOCK_EPS = 1e-6
OUTER_EPS = 1e-5

F32 = mybir.dt.float32
F32R = mybir.dt.float32r
I32 = mybir.dt.int32
ALU = mybir.AluOpType
ACT = mybir.ActivationFunctionType
AX = mybir.AxisListType

WQ, WK, WV, WO, W1, W2 = 0, P, 2 * P, 3 * P, 4 * P, 4 * P + FF
PAR = W2 + FF
BQ, BK, BV, BO, LN1S, LN1B, B2, LN2S, LN2B, B1 = range(10)
NPAR = B1 + FT
LAYER_COLS = PAR + NPAR
QKV = 3 * P

NEWTON_ROUNDS = 3
RSQRT_STEPS = 3 + 3 * NEWTON_ROUNDS
FOLD_STEPS = 7

RING = 3
LEFT_OUT = [("none", 0), ("none", 1)]
LAYER_ORDER = [(t, p) for p in range(PAIRS) for t in ("k", "v", "q")] + LEFT_OUT
LAYER_ORDER += [("o", p) for p in range(PAIRS)]
LAYER_ORDER += [("c0", p) for p in range(PAIRS)] + [("r0", 0), ("r0", 1)]
LAYER_ORDER += [("h", 0, j) for j in range(FT)] + [("r0", 2), ("r0", 3)]
LAYER_ORDER += [("h", 1, j) for j in range(FT)] + [("f", 0)]
LAYER_ORDER += [("h", 2, j) for j in range(FT)] + [("f", 1), ("c1", 0)]
LAYER_ORDER += [("h", 3, j) for j in range(FT)] + [("c1", 1), ("f", 2), ("r1", 0), ("r1", 1)]
LAYER_ORDER += [("f", 3), ("c1", 2), ("c1", 3), ("r1", 2), ("r1", 3)]
assert len(LAYER_ORDER) % RING == 0
SLOT = {key: n % RING for n, key in enumerate(LAYER_ORDER)}

LAST_ORDER = [("c0", p) for p in range(PAIRS)] + [("r0", p) for p in range(PAIRS)]
for _p in range(PAIRS):
    LAST_ORDER += [("h", _p, j) for j in range(FT)] + [("f", _p)]
LAST_ORDER += [("rf", p) for p in range(PAIRS)]
LAST_ORDER += [("c1", p) for p in range(PAIRS)] + [("r1", p) for p in range(PAIRS)]
LAST_SLOT = {key: n % RING for n, key in enumerate(LAST_ORDER)}


def before(key, last):
    order = LAST_ORDER if last else LAYER_ORDER
    n = order.index(key) - RING
    while n >= 0 and order[n] in LEFT_OUT:
        n -= RING
    return (order[n], False) if n >= 0 else (LAYER_ORDER[len(LAYER_ORDER) + n], True)


def build(nc, x_in, layers_in, fc_in, proj_in, ffn_ln_in, out):
    with ExitStack() as ctx:
        def sb(name, shape, dt=F32):
            return ctx.enter_context(nc.sbuf_tensor(name, shape, dt))

        def sem(name):
            return ctx.enter_context(nc.semaphore(name))

        x0 = sb("x0", [P, TOKENS])
        x = sb("x", [P, TOKENS])
        xh = sb("xh", [P, TOKENS], F32R)
        xl = sb("xl", [P, TOKENS], F32R)
        y = sb("y", [P, TOKENS])
        s = y
        yc = sb("yc", [P, TOKENS])
        h = sb("h", [P, 2, FT * PAIR])
        sq = sb("sq", [P, 2, PAIR])
        a = sb("a", [P, 2, PAIR])
        kw = sb("kw", [P, 2, PAIR])
        qw = sb("qw", [P, 2, PAIR])
        kk = sb("kk", [P, PAIR])
        raw = sb("raw", [P, LAYER_COLS])
        wh = sb("wh", [P, QKV + FF], F32R)
        wl = sb("wl", [P, QKV + FF], F32R)
        w2 = sb("w2", [P, FF])
        wo = sb("wo", [P, BATCHES, P])
        par = sb("par", [P, NPAR])
        bk1 = sb("bk1", [P, 2])
        bq1 = sb("bq1", [P, 1])
        ksum = sb("ksum", [P, PAIRS])
        kvsum = sb("kvsum", [P, PAIRS])
        fold = sb("fold", [P, FOLD_STEPS, BATCHES])
        bias_o = sb("bias_o", [P, BATCHES])
        vv = sb("vv", [ROWS, ROW])
        ti = sb("ti", [ROWS, ROW], I32)
        tf = sb("tf", [ROWS, ROW])
        ry = sb("ry", [ROWS, ROW])
        mu = sb("mu", [ROWS, ROW])
        rr = sb("rr", [LOW + ROWS, BATCHES, ROW], F32R)
        center = sb("center", [P, P])
        slide = sb("slide", [P, 2 * ROWS - 1])
        slide_ff = sb("slide_ff", [P, 2 * ROWS - 1])
        ones = sb("ones", [P, P])
        ones_ff = sb("ones_ff", [P, P])
        pick = sb("pick", [LOW + ROWS, ROWS, P], F32R)
        fc = sb("fc", [P, FF])
        proj = sb("proj", [P, FF])
        ffn_ln = sb("ffn_norm", [P, 2 * FT])
        tern = sb("tern", [P, FF])
        tfc = sb("tfc", [P, FF], F32R)
        tpj = sb("tpj", [P, FF])
        gam = sb("gam", [P, 2, 4])
        pw = sb("pw", [P, FF])
        cb = sb("cb", [P, 1])

        tile = [ctx.enter_context(nc.psum_tensor(f"tile{n}", [P, PAIR], F32)) for n in range(RING)]
        stat = ctx.enter_context(nc.psum_tensor("stat", [P, BANK], F32))
        small = ctx.enter_context(nc.psum_tensor("small", [P, BANK], F32))

        x0_in, x_in_s, w_in, ffn_in, stored = (sem(n) for n in ("x0_in", "x_in_s", "w_in", "ffn_in", "stored"))
        const_ready, zero_ready, y_ready, g_part = (sem(n) for n in ("const_ready", "zero_ready", "y_ready", "g_part"))
        k_mm, v_mm, q_mm, o_mm, fold_mm, c_mm, var_mm, r_mm, h_mm, f_mm, gam_mm, pw_mm, rf_mm, st_mm = (
            sem(n) for n in ("k_mm", "v_mm", "q_mm", "o_mm", "fold_mm", "c_mm", "var_mm", "r_mm", "h_mm", "f_mm",
                             "gam_mm", "pw_mm", "rf_mm", "st_mm"))
        k_neg, k_exp, q_exp, s_ln, s_ready, g_once, a_ready, h_ready, sq_ready, yc_ready, g_sq, p_out = (
            sem(n) for n in ("k_neg", "k_exp", "q_exp", "s_ln", "s_ready", "g_once", "a_ready", "h_ready",
                             "sq_ready", "yc_ready", "g_sq", "p_out"))
        par_ready, w_hi, w_lo, w2_ready, b_ready = (
            sem(n) for n in ("par_ready", "w_hi", "w_lo", "w2_ready", "b_ready"))
        k_round, k_ready, kv_ready, q_neg, q_round, q_max, folded, bias_ready = (
            sem(n) for n in ("k_round", "k_ready", "kv_ready", "q_neg", "q_round", "q_max", "folded",
                             "bias_ready"))
        rsqrt, r_ready, x_norm, x_new, x_hi, x_lo, tern_step, gam_step, s_sum, moment, y_step = (
            sem(n) for n in ("rsqrt", "r_ready", "x_norm", "x_new", "x_hi", "x_lo", "tern_step", "gam_step",
                             "s_sum", "moment", "y_step"))

        def cols(p):
            return slice(p * PAIR, (p + 1) * PAIR)

        def slot_of(key, last=False):
            return (LAST_SLOT if last else SLOT)[key]

        def reader(i, key, last):
            t, p = key[0], key[1]
            if t == "h":
                return h_ready, i * PAIRS * FT + p * FT + key[2] + 1
            if last and t in ("f", "rf"):
                return (p_out if t == "f" else y_step), p + 1
            if t == "f":
                return a_ready, i * 2 * PAIRS + PAIRS + p + 1
            if t[0] in "cr":
                return (sq_ready if t[0] == "c" else x_norm), i * 2 * PAIRS + int(t[1]) * PAIRS + p + 1
            return {"k": k_ready, "v": kv_ready, "q": q_max, "o": g_once}[t], i * PAIRS + p + 1

        block = ctx.enter_context(nc.Block())

        @block.sync
        def _(sp):
            sp.dma_start(raw[:, :], layers_in[0]).then_inc(w_in, 16)
            for p in range(PAIRS):
                sp.dma_start(x[:, cols(p)], x_in[:, cols(p)]).then_inc(x_in_s, 16)
            sp.dma_start(fc[:, :], fc_in).then_inc(ffn_in, 16)
            sp.dma_start(proj[:, :], proj_in).then_inc(ffn_in, 16)
            sp.dma_start(ffn_ln[:, :], ffn_ln_in).then_inc(ffn_in, 16)
            sp.dma_start(x0[:, :], x_in).then_inc(x0_in, 16)
            with sp.Fori(1, LAYERS) as i:
                sp.wait_ge(bias_ready, i * BATCHES)
                sp.dma_start(raw[:, :], layers_in[bass.ds(i, 1), :, :].rearrange("a p n -> (a p) n")).then_inc(w_in, 16)
            for p in range(PAIRS):
                sp.wait_ge(x_norm, 2 * PAIRS * LAYERS + PAIRS + p + 1)
                sp.dma_start(out[:, cols(p)], x[:, cols(p)]).then_inc(stored, 16)
            sp.wait_ge(stored, 16 * PAIRS)

        @block.gpsimd
        def _(pool):
            pool.memset(center[:, :], -1.0 / P).then_inc(zero_ready, 1)
            pool.memset(slide[:, :], 0.0).then_inc(zero_ready, 1)
            pool.memset(slide_ff[:, :], 0.0).then_inc(zero_ready, 1)
            pool.memset(pick[:, :, :].bitcast(F32), 0.0).then_inc(zero_ready, 1)
            pool.memset(rr[:, :, :].bitcast(F32), 0.0).then_inc(const_ready, 1)
            pool.memset(ones[:, :], 1.0).then_inc(const_ready, 1)
            pool.memset(ones_ff[:, :], 1.0 / FF).then_inc(const_ready, 1)
            pool.wait_ge(zero_ready, 4)
            pool.affine_select(out=center[:, :], in_=center[:, :], compare_op=ALU.not_equal, fill=1.0 - 1.0 / P,
                               base=0, pattern=[[-1, P]], channel_multiplier=1).then_inc(const_ready, 1)
            pool.memset(slide[:, ROWS - 1:ROWS], 1.0 / P).then_inc(const_ready, 1)
            pool.memset(slide_ff[:, ROWS - 1:ROWS], 1.0 / FF).then_inc(const_ready, 1)
            pool.affine_select(out=pick[:, :, :], in_=pick[:, :, :], compare_op=ALU.not_equal, fill=1.0,
                               base=0, pattern=[[-1, ROWS], [0, P]], channel_multiplier=1).then_inc(zero_ready, 1)
            pool.wait_ge(zero_ready, 5)
            pool.affine_select(out=pick[:, :, :], in_=pick[:, :, :], compare_op=ALU.not_equal, fill=1.0,
                               base=-LOW, pattern=[[-1, ROWS], [0, P]], channel_multiplier=1).then_inc(const_ready, 1)
            with pool.Fori(0, LAYERS) as i:
                for n in range(2):
                    for p in range(PAIRS):
                        pool.wait_ge(a_ready, i * 2 * PAIRS + n * PAIRS + p + 1)
                        pool.tensor_tensor(y[:, cols(p)], a[:, p % 2, :], x[:, cols(p)], ALU.add).then_inc(y_ready, 1)
            pool.wait_ge(x0_in, 16)
            for p in range(PAIRS):
                pool.wait_ge(x_new, 2 * PAIRS * (LAYERS - 1) + PAIRS + p + 1)
                pool.tensor_tensor(y[:, cols(p)], x0[:, cols(p)], x[:, cols(p)], ALU.add).then_inc(y_ready, 1)
            for p in range(PAIRS):
                pool.wait_ge(h_ready, LAYERS * PAIRS * FT + p * FT + 2)
                if p >= 2:
                    pool.wait_ge(st_mm, 2 * (p - 1))
                pool.tensor_tensor(kw[:, p % 2, :], h[:, p % 2, 0:PAIR], h[:, p % 2, PAIR:2 * PAIR],
                                   ALU.add).then_inc(g_part, 1)
                for j in range(2, FT):
                    pool.wait_ge(h_ready, LAYERS * PAIRS * FT + p * FT + j + 1)
                    pool.wait_ge(g_part, p * (FT - 1) + j - 1)
                    pool.tensor_tensor(kw[:, p % 2, :], kw[:, p % 2, :], h[:, p % 2, j * PAIR:(j + 1) * PAIR],
                                       ALU.add).then_inc(g_part, 1)

        @block.scalar
        def _(act):
            def squares(base, n, p, last=False):
                m = n * PAIRS + p
                slot = slot_of((f"c{n}", p), last)
                act.wait_ge(c_mm, base + m + 1)
                if m >= 2:
                    act.wait_ge(var_mm, base + m - 1)
                act.activation(yc[:, cols(p)], tile[slot][:, :], ACT.Copy).then_inc(yc_ready, 1)
                act.activation(sq[:, p % 2, :], tile[slot][:, :], ACT.Square).then_inc(sq_ready, 1)

            def hidden(base_h, base_f, p, func, bias, last=False):
                for j in range(FT):
                    slot = slot_of(("h", p, j), last)
                    act.wait_ge(h_mm, base_h + p * FT + j + 1)
                    if p >= 2 and j == 0:
                        act.wait_ge(f_mm, base_f + p - 1)
                    act.activation(h[:, p % 2, j * PAIR:(j + 1) * PAIR], tile[slot][:, :], func,
                                   bias=bias(j)).then_inc(h_ready, 1)

            act.wait_ge(const_ready, 7)
            with act.Fori(0, LAYERS) as i:
                act.wait_ge(b_ready, 3 * (i + 1))

                def exps(p):
                    slot = slot_of(("k", p))
                    act.wait_ge(k_mm, i * PAIRS + p + 1)
                    if p >= 2:
                        act.wait_ge(k_ready, i * PAIRS + p - 1)
                    act.activation(kw[:, p % 2, :], tile[slot][:, :], ACT.Relu, bias=bk1[:, 0:1],
                                   scale=-1.0).then_inc(k_neg, 1)
                    act.wait_ge(k_neg, i * PAIRS + p + 1)
                    act.activation(kw[:, p % 2, :], kw[:, p % 2, :], ACT.Exp, scale=-1.0).then_inc(k_exp, 1)
                    act.wait_ge(q_neg, i * PAIRS + p + 1)
                    act.activation(qw[:, p % 2, :], qw[:, p % 2, :], ACT.Exp).then_inc(q_exp, 1)

                def shares(p):
                    n = p // PAIRS_PER_BATCH
                    act.wait_ge(folded, i * FOLD_STEPS * BATCHES + n * FOLD_STEPS + 3)
                    act.wait_ge(q_max, i * PAIRS + p + 1)
                    act.activation(s[:, cols(p)], s[:, cols(p)], ACT.Ln, bias=1.0,
                                   scale=fold[:, 2, n:n + 1]).then_inc(s_ln, 1)
                    act.wait_ge(s_ln, i * PAIRS + p + 1)
                    act.activation(s[:, cols(p)], s[:, cols(p)], ACT.Exp, scale=-1.0).then_inc(s_ready, 1)

                def gelu_once(p):
                    slot = slot_of(("o", p))
                    n = p // PAIRS_PER_BATCH
                    act.wait_ge(o_mm, i * PAIRS + p + 1)
                    act.wait_ge(bias_ready, i * BATCHES + n + 1)
                    if p >= 2:
                        act.wait_ge(y_ready, i * 2 * PAIRS + p - 1)
                    act.activation(a[:, p % 2, :], tile[slot][:, :], ACT.Gelu_apprx_tanh,
                                   bias=bias_o[:, n:n + 1]).then_inc(g_once, 1)

                def gelu_twice(p):
                    slot = slot_of(("o", p))
                    act.wait_ge(g_once, i * PAIRS + p + 1)
                    act.activation(a[:, p % 2, :], a[:, p % 2, :], ACT.Gelu_apprx_tanh).then_inc(a_ready, 1)

                def gelu_out(p):
                    slot = slot_of(("f", p))
                    act.wait_ge(f_mm, i * PAIRS + p + 1)
                    act.wait_ge(y_ready, i * 2 * PAIRS + PAIRS + p - 1)
                    act.activation(a[:, p % 2, :], tile[slot][:, :], ACT.Gelu_apprx_tanh,
                                   bias=par[:, B2:B2 + 1]).then_inc(a_ready, 1)

                for p in range(PAIRS):
                    exps(p)
                    if p >= PAIRS_PER_BATCH:
                        shares(p - PAIRS_PER_BATCH)
                for p in range(PAIRS_PER_BATCH, PAIRS):
                    shares(p)
                for p in range(PAIRS + 1):
                    if p < PAIRS:
                        gelu_once(p)
                    if p >= 1:
                        gelu_twice(p - 1)
                for p in range(PAIRS):
                    squares(i * 2 * PAIRS, 0, p)
                layer_hidden = lambda p: hidden(i * PAIRS * FT, i * PAIRS, p, ACT.Gelu_apprx_tanh,
                                                lambda j: par[:, B1 + j:B1 + j + 1])
                layer_hidden(0)
                layer_hidden(1)
                gelu_out(0)
                layer_hidden(2)
                gelu_out(1)
                squares(i * 2 * PAIRS, 1, 0)
                layer_hidden(3)
                squares(i * 2 * PAIRS, 1, 1)
                gelu_out(2)
                gelu_out(3)
                squares(i * 2 * PAIRS, 1, 2)
                squares(i * 2 * PAIRS, 1, 3)

            for p in range(PAIRS):
                squares(LAYERS * 2 * PAIRS, 0, p, last=True)
            for p in range(PAIRS):
                hidden(LAYERS * PAIRS * FT, LAYERS * PAIRS, p, ACT.Gelu, lambda j: 0.0, last=True)
                for j in range(FT):
                    act.wait_ge(h_ready, LAYERS * PAIRS * FT + p * FT + j + 1)
                    if j == 0:
                        if p >= 2:
                            act.wait_ge(st_mm, 2 * (p - 1))
                        act.activation(a[:, p % 2, :], h[:, p % 2, 0:PAIR], ACT.Square).then_inc(g_sq, 1)
                        continue
                    done = p * (FT - 1) + j - 2
                    if done > 0:
                        act.wait_ge(s_sum, done)
                    act.activation(qw[:, (p * (FT - 1) + j - 1) % 2, :], h[:, p % 2, j * PAIR:(j + 1) * PAIR],
                                   ACT.Square).then_inc(g_sq, 1)
                slot = slot_of(("f", p), True)
                act.wait_ge(f_mm, LAYERS * PAIRS + p + 1)
                act.activation(yc[:, cols(p)], tile[slot][:, :], ACT.Copy).then_inc(p_out, 1)
                act.wait_ge(p_out, p + 1)
            for p in range(PAIRS):
                squares(LAYERS * 2 * PAIRS, 1, p, last=True)

        @block.vector
        def _(dve):
            def rsqrt_of(call, n, eps, ready=None):
                base = call * RSQRT_STEPS
                if ready is None:
                    dve.tensor_scalar(vv[:, :], stat[0:ROWS, 0:ROW], eps, None, ALU.add).then_inc(rsqrt, 1)
                else:
                    ready(rsqrt)
                dve.wait_ge(rsqrt, base + 1)
                dve.tensor_scalar(ti[:, :], vv[:, :].bitcast(I32), 1, None, ALU.logical_shift_right).then_inc(rsqrt, 1)
                dve.wait_ge(rsqrt, base + 2)
                dve.tensor_scalar(ry[:, :].bitcast(I32), ti[:, :], -1.0, float(0x5F3759DF), ALU.mult,
                                  ALU.add).then_inc(rsqrt, 1)
                for r in range(NEWTON_ROUNDS):
                    dve.wait_ge(rsqrt, base + 3 + 3 * r)
                    dve.tensor_tensor(tf[:, :], ry[:, :], ry[:, :], ALU.mult).then_inc(rsqrt, 1)
                    dve.wait_ge(rsqrt, base + 4 + 3 * r)
                    dve.scalar_tensor_tensor(tf[:, :], tf[:, :], -0.5, vv[:, :], ALU.mult, ALU.mult).then_inc(rsqrt, 1)
                    dve.wait_ge(rsqrt, base + 5 + 3 * r)
                    dve.scalar_tensor_tensor(ry[:, :], tf[:, :], 1.5, ry[:, :], ALU.add, ALU.mult).then_inc(rsqrt, 1)
                dve.wait_ge(rsqrt, base + RSQRT_STEPS)
                dve.tensor_copy(rr[0:ROWS, n, :], ry[:, :]).then_inc(r_ready, 1)
                dve.wait_ge(r_ready, 2 * call + 1)
                dve.tensor_tensor(rr[LOW:LOW + ROWS, n, :], ry[:, :], rr[0:ROWS, n, :].bitcast(F32),
                                  ALU.subtract).then_inc(r_ready, 1)

            def split_x(m, p):
                dve.tensor_copy(xh[:, cols(p)], x[:, cols(p)]).then_inc(x_hi, 1)
                dve.wait_ge(x_hi, m + 1)
                dve.tensor_tensor(xl[:, cols(p)], x[:, cols(p)], xh[:, cols(p)].bitcast(F32),
                                  ALU.subtract).then_inc(x_lo, 1)

            def normed(base, n, p, scale, shift, last=False, split=True):
                m = n * PAIRS + p
                slot = slot_of((f"r{n}", p), last)
                dve.wait_ge(r_mm, base + m + 1)
                dve.wait_ge(yc_ready, base + m + 1)
                dve.scalar_tensor_tensor(x[:, cols(p)], yc[:, cols(p)], scale, tile[slot][:, :], ALU.mult,
                                         ALU.mult).then_inc(x_norm, 1)
                dve.wait_ge(x_norm, base + m + 1)
                if shift is not None:
                    dve.tensor_scalar(x[:, cols(p)], x[:, cols(p)], shift, None, ALU.add).then_inc(x_new, 1)
                    dve.wait_ge(x_new, base + m + 1)
                if split:
                    split_x(base + PAIRS + m, p)

            for p in range(PAIRS):
                dve.wait_ge(x_in_s, 16 * PAIRS)
                split_x(p, p)

            dve.wait_ge(ffn_in, 48)
            for n, w in enumerate((fc, proj)):
                dve.tensor_reduce(gam[:, n, 0:1], w[:, :], AX.X, ALU.add, apply_absolute_value=True).then_inc(gam_step, 1)
            dve.wait_ge(gam_mm, 1)
            for n, (w, t) in enumerate(((fc, tfc), (proj, tpj))):
                dve.tensor_scalar(gam[:, n, 1:2], small[:, n:n + 1], 1.0 / (P * FF), 1e-6, ALU.mult,
                                  ALU.add).then_inc(tern_step, 1)
                dve.wait_ge(tern_step, 5 * n + 1)
                dve.tensor_scalar(gam[:, n, 2:3], gam[:, n, 1:2], 0.5, None, ALU.mult).then_inc(tern_step, 1)
                dve.tensor_scalar(gam[:, n, 3:4], gam[:, n, 1:2], -0.5, None, ALU.mult).then_inc(tern_step, 1)
                dve.wait_ge(tern_step, 5 * n + 3)
                dve.tensor_scalar(tern[:, :], w[:, :], gam[:, n, 3:4], None, ALU.is_lt).then_inc(tern_step, 1)
                dve.wait_ge(tern_step, 5 * n + 4)
                dve.scalar_tensor_tensor(t[:, :], w[:, :], gam[:, n, 2:3], tern[:, :], ALU.is_gt,
                                         ALU.subtract).then_inc(tern_step, 1)
                dve.wait_ge(tern_step, 5 * n + 5)
            for j in range(FT):
                dve.tensor_scalar(pw[:, j * P:(j + 1) * P], tpj[:, j * P:(j + 1) * P], ffn_ln[:, j:j + 1], None,
                                  ALU.mult).then_inc(gam_step, 1)
            dve.wait_ge(gam_step, 2 + FT)
            dve.wait_ge(pw_mm, 1)
            for j in range(FT):
                dve.tensor_tensor(pw[:, j * P:(j + 1) * P], pw[:, j * P:(j + 1) * P], small[:, P:2 * P],
                                  ALU.subtract).then_inc(gam_step, 1)
            dve.tensor_copy(cb[:, :], small[:, 2 * P:2 * P + 1]).then_inc(gam_step, 1)

            with dve.Fori(0, LAYERS) as i:
                dve.wait_ge(w_in, 16 * (i + 1))
                dve.tensor_copy(par[:, :], raw[:, PAR:PAR + NPAR]).then_inc(par_ready, 1)
                dve.tensor_copy(wh[:, 0:QKV], raw[:, 0:QKV]).then_inc(w_hi, 1)
                dve.wait_ge(w_hi, 2 * i + 1)
                dve.tensor_tensor(wl[:, 0:QKV], raw[:, 0:QKV], wh[:, 0:QKV].bitcast(F32), ALU.subtract).then_inc(w_lo, 1)
                dve.wait_ge(par_ready, i + 1)
                dve.tensor_scalar(bk1[:, 0:1], par[:, BK:BK + 1], -1.0, None, ALU.mult).then_inc(b_ready, 1)
                dve.tensor_scalar(bk1[:, 1:2], par[:, BK:BK + 1], 1.0, None, ALU.add).then_inc(b_ready, 1)
                dve.tensor_scalar(bq1[:, :], par[:, BQ:BQ + 1], 1.0, None, ALU.add).then_inc(b_ready, 1)
                dve.tensor_copy(wh[:, QKV:], raw[:, W1:W1 + FF]).then_inc(w_hi, 1)
                dve.wait_ge(w_hi, 2 * i + 2)
                dve.tensor_tensor(wl[:, QKV:], raw[:, W1:W1 + FF], wh[:, QKV:].bitcast(F32), ALU.subtract).then_inc(w_lo, 1)
                dve.tensor_copy(w2[:, :], raw[:, W2:W2 + FF]).then_inc(w2_ready, 1)
                dve.wait_ge(b_ready, 3 * (i + 1))

                def sums(p):
                    m = i * PAIRS + p
                    k_slot, v_slot, q_slot = (slot_of((t, p)) for t in "kvq")
                    dve.wait_ge(k_exp, m + 1)
                    dve.tensor_scalar(kw[:, p % 2, :], kw[:, p % 2, :], -1.0, 1.0, ALU.add, ALU.add).then_inc(k_round, 1)
                    dve.wait_ge(k_round, m + 1)
                    if p >= 1:
                        dve.wait_ge(kv_ready, m)
                    dve.scalar_tensor_tensor(kk[:, :], tile[k_slot][:, :], bk1[:, 1:2], kw[:, p % 2, :], ALU.add,
                                             ALU.max, accum_out=ksum[:, p:p + 1]).then_inc(k_ready, 1)
                    dve.wait_ge(q_mm, m + 1)
                    if p >= 2:
                        dve.wait_ge(q_max, m - 1)
                    dve.tensor_scalar(qw[:, p % 2, :], tile[q_slot][:, :], par[:, BQ:BQ + 1], 0.0, ALU.add,
                                      ALU.min).then_inc(q_neg, 1)
                    dve.wait_ge(k_ready, m + 1)
                    dve.wait_ge(v_mm, m + 1)
                    dve.scalar_tensor_tensor(kk[:, :], tile[v_slot][:, :], par[:, BV:BV + 1], kk[:, :], ALU.add,
                                             ALU.mult, accum_out=kvsum[:, p:p + 1]).then_inc(kv_ready, 1)
                    dve.wait_ge(q_exp, m + 1)
                    dve.tensor_scalar(qw[:, p % 2, :], qw[:, p % 2, :], -1.0, 1.0, ALU.add, ALU.add).then_inc(q_round, 1)
                    dve.wait_ge(kv_ready, m + 1)
                    dve.wait_ge(q_round, m + 1)
                    dve.scalar_tensor_tensor(s[:, cols(p)], tile[q_slot][:, :], bq1[:, 0:1], qw[:, p % 2, :], ALU.add,
                                             ALU.max).then_inc(q_max, 1)
                    dve.wait_ge(q_max, m + 1)

                def fold_kv(n):
                    base = i * FOLD_STEPS * BATCHES + n * FOLD_STEPS
                    b = slice(n, n + 1)
                    p = n * PAIRS_PER_BATCH
                    dve.tensor_tensor(fold[:, 0, b], ksum[:, p:p + 1], ksum[:, p + 1:p + 2], ALU.add).then_inc(folded, 1)
                    dve.tensor_tensor(fold[:, 1, b], kvsum[:, p:p + 1], kvsum[:, p + 1:p + 2], ALU.add).then_inc(folded, 1)
                    dve.wait_ge(folded, base + 2)
                    dve.tensor_scalar(fold[:, 2, b], fold[:, 0, b], 1.0 / ZEPS, None, ALU.mult).then_inc(folded, 1)
                    dve.tensor_scalar(fold[:, 3, b], fold[:, 0, b], 2.0 ** -30, None, ALU.max).then_inc(folded, 1)
                    dve.wait_ge(folded, base + 4)
                    dve.reciprocal(fold[:, 4, b], fold[:, 3, b]).then_inc(folded, 1)
                    dve.wait_ge(folded, base + 5)
                    dve.tensor_tensor(fold[:, 5, b], fold[:, 1, b], fold[:, 4, b], ALU.mult).then_inc(folded, 1)
                    dve.wait_ge(folded, base + 6)
                    dve.tensor_scalar(wo[:, n, :], raw[:, WO:WO + P], fold[:, 5, b], -1.0, ALU.mult,
                                      ALU.mult).then_inc(folded, 1)

                for p in range(PAIRS):
                    sums(p)
                    if p % PAIRS_PER_BATCH == PAIRS_PER_BATCH - 1:
                        fold_kv(p // PAIRS_PER_BATCH)
                for n in range(BATCHES):
                    dve.wait_ge(fold_mm, i * BATCHES + n + 1)
                    dve.tensor_tensor(bias_o[:, n:n + 1], small[:, n:n + 1], par[:, BO:BO + 1], ALU.add).then_inc(bias_ready, 1)
                for n, (sc, sh) in enumerate(((LN1S, LN1B), (LN2S, LN2B))):
                    for b in range(BATCHES):
                        dve.wait_ge(var_mm, i * 2 * PAIRS + n * PAIRS + (b + 1) * PAIRS_PER_BATCH)
                        rsqrt_of(i * 2 * BATCHES + n * BATCHES + b, b, BLOCK_EPS)
                        for p in range(b * PAIRS_PER_BATCH, (b + 1) * PAIRS_PER_BATCH):
                            normed(i * 2 * PAIRS, n, p, par[:, sc:sc + 1], par[:, sh:sh + 1])

            def outer(n, b, split):
                base = LAYERS * 2 * PAIRS
                dve.wait_ge(var_mm, base + n * PAIRS + (b + 1) * PAIRS_PER_BATCH)
                rsqrt_of(LAYERS * 2 * BATCHES + 2 * n * BATCHES + b, b, OUTER_EPS)
                for p in range(b * PAIRS_PER_BATCH, (b + 1) * PAIRS_PER_BATCH):
                    normed(base, n, p, 1.0, None, last=True, split=split)

            for b in range(BATCHES):
                outer(0, b, True)
            for p in range(PAIRS):
                for j in range(1, FT):
                    m = p * (FT - 1) + j - 1
                    dve.wait_ge(g_sq, p * FT + j + 1)
                    if m > 0:
                        dve.wait_ge(s_sum, m)
                    dve.tensor_tensor(a[:, p % 2, :], a[:, p % 2, :], qw[:, m % 2, :], ALU.add).then_inc(s_sum, 1)
                if p % PAIRS_PER_BATCH == PAIRS_PER_BATCH - 1:
                    b = p // PAIRS_PER_BATCH
                    dve.wait_ge(st_mm, 2 * (p + 1))

                    def variance(done):
                        dve.tensor_copy(mu[:, :], stat[0:ROWS, 0:ROW]).then_inc(moment, 1)
                        dve.tensor_scalar(vv[:, :], small[0:ROWS, 0:ROW], OUTER_EPS, None, ALU.add).then_inc(moment, 1)
                        dve.wait_ge(moment, 3 * b + 2)
                        dve.tensor_tensor(mu[:, :], mu[:, :], mu[:, :], ALU.mult).then_inc(moment, 1)
                        dve.wait_ge(moment, 3 * b + 3)
                        dve.tensor_tensor(vv[:, :], vv[:, :], mu[:, :], ALU.subtract).then_inc(done, 1)

                    rsqrt_of((LAYERS * 2 + 1) * BATCHES + b, b, OUTER_EPS, variance)
            for p in range(PAIRS):
                slot = slot_of(("rf", p), True)
                dve.wait_ge(rf_mm, p + 1)
                dve.wait_ge(p_out, p + 1)
                dve.tensor_tensor(yc[:, cols(p)], yc[:, cols(p)], tile[slot][:, :], ALU.mult).then_inc(y_step, 1)
                dve.wait_ge(y_step, p + 1)
                dve.scalar_tensor_tensor(y[:, cols(p)], yc[:, cols(p)], cb[:, 0:1], x[:, cols(p)], ALU.add,
                                         ALU.add).then_inc(y_ready, 1)
            for b in range(BATCHES):
                outer(1, b, False)

        @block.tensor
        def _(pe):
            def halves(slot):
                return [(tile[slot][:, c * BANK:(c + 1) * BANK], c * BANK) for c in range(PAIR // BANK)]

            def free(i, key, last=False):
                earlier, wrapped = before(key, last)
                if wrapped and earlier[0] == "r1":
                    pe.wait_ge(x_hi, i * 2 * PAIRS + earlier[1] + 1)
                elif wrapped:
                    assert earlier[0] == "c1"
                else:
                    pe.wait_ge(*reader(i, earlier, last))
                return slot_of(key, last)

            def product(slot, w0, p, done):
                for dst, at in halves(slot):
                    t = slice(p * PAIR + at, p * PAIR + at + BANK)
                    pe.matmul(dst, wh[:, w0:w0 + P], xh[:, t], start=True, stop=False)
                    pe.matmul(dst, wh[:, w0:w0 + P], xl[:, t], start=False, stop=False)
                    mm = pe.matmul(dst, wl[:, w0:w0 + P], xh[:, t], start=False, stop=True)
                mm.then_inc(done, 1)

            def centered(base, i, n, p, last=False):
                m = n * PAIRS + p
                slot = free(i, (f"c{n}", p), last)
                pe.wait_ge(y_ready, base + m + 1)
                for dst, at in halves(slot):
                    mm = pe.matmul(dst, center[:, :], y[:, p * PAIR + at:p * PAIR + at + BANK], start=True, stop=True)
                mm.then_inc(c_mm, 1)

            def variances(base, calls, n, p):
                m = n * PAIRS + p
                first, last = p % PAIRS_PER_BATCH == 0, p % PAIRS_PER_BATCH == PAIRS_PER_BATCH - 1
                pe.wait_ge(sq_ready, base + m + 1)
                if first and calls is not None:
                    pe.wait_ge(rsqrt, calls)
                for r in range(ROWS_PER_PAIR):
                    row = (p % PAIRS_PER_BATCH) * ROWS_PER_PAIR + r
                    mm = pe.matmul(stat[0:ROWS, 0:ROW], slide[:, ROWS - 1 - row:2 * ROWS - 1 - row],
                                   sq[:, p % 2, r * ROW:(r + 1) * ROW], start=first and r == 0,
                                   stop=last and r == ROWS_PER_PAIR - 1)
                mm.then_inc(var_mm, 1)

            def spread(slot, p, call, done):
                pe.wait_ge(r_ready, 2 * (call + 1))
                for r in range(ROWS_PER_PAIR):
                    row = (p % PAIRS_PER_BATCH) * ROWS_PER_PAIR + r
                    mm = pe.matmul(tile[slot][:, r * ROW:(r + 1) * ROW], pick[:, row, :],
                                   rr[:, p // PAIRS_PER_BATCH, :], start=True, stop=True)
                mm.then_inc(done, 1)

            pe.wait_ge(const_ready, 7)
            pe.wait_ge(gam_step, 2)
            for n in range(2):
                mm = pe.matmul(small[:, n:n + 1], ones[:, :], gam[:, n, 0:1], start=True, stop=True)
            mm.then_inc(gam_mm, 1)
            pe.wait_ge(gam_step, 2 + FT)
            for j in range(FT):
                pe.matmul(small[:, P:2 * P], ones_ff[:, :], pw[:, j * P:(j + 1) * P], start=(j == 0), stop=(j == FT - 1))
            for j in range(FT):
                mm = pe.matmul(small[:, 2 * P:2 * P + 1], tpj[:, j * P:(j + 1) * P], ffn_ln[:, FT + j:FT + j + 1],
                               start=(j == 0), stop=(j == FT - 1))
            mm.then_inc(pw_mm, 1)
            pe.wait_ge(gam_step, 2 + 2 * FT + 1)

            with pe.Fori(0, LAYERS) as i:
                base = i * 2 * PAIRS

                def fold_bias(n):
                    pe.wait_ge(folded, i * FOLD_STEPS * BATCHES + (n + 1) * FOLD_STEPS)
                    if n > 0:
                        pe.wait_ge(bias_ready, i * BATCHES + n)
                    pe.matmul(small[:, n:n + 1], raw[:, WO:WO + P], fold[:, 5, n:n + 1], start=True,
                              stop=True).then_inc(fold_mm, 1)

                def attn_out(p):
                    slot = free(i, ("o", p))
                    pe.wait_ge(s_ready, i * PAIRS + p + 1)
                    for dst, at in halves(slot):
                        mm = pe.matmul(dst, wo[:, p // PAIRS_PER_BATCH, :], s[:, p * PAIR + at:p * PAIR + at + BANK],
                                       start=True, stop=True)
                    mm.then_inc(o_mm, 1)

                def up(p):
                    if p == 0:
                        pe.wait_ge(w_lo, 2 * i + 2)
                        pe.wait_ge(w2_ready, i + 1)
                    pe.wait_ge(x_lo, base + PAIRS + p + 1)
                    for j in range(FT):
                        product(free(i, ("h", p, j)), QKV + j * P, p, h_mm)

                def down(p):
                    slot = free(i, ("f", p))
                    pe.wait_ge(h_ready, i * PAIRS * FT + (p + 1) * FT)
                    for dst, at in halves(slot):
                        for j in range(FT):
                            mm = pe.matmul(dst, w2[:, j * P:(j + 1) * P],
                                           h[:, p % 2, j * PAIR + at:j * PAIR + at + BANK], start=(j == 0),
                                           stop=(j == FT - 1))
                    mm.then_inc(f_mm, 1)

                def rstd(n, p):
                    spread(free(i, (f"r{n}", p)), p, i * 2 * BATCHES + n * BATCHES + p // PAIRS_PER_BATCH, r_mm)

                def stats(n, p):
                    call = i * 2 * BATCHES + n * BATCHES + p // PAIRS_PER_BATCH
                    calls = None
                    if n > 0 or p >= PAIRS_PER_BATCH:
                        calls = (call - 1) * RSQRT_STEPS + 1
                    variances(base, calls, n, p)

                pe.wait_ge(w_lo, 2 * i + 1)
                for p in range(PAIRS):
                    pe.wait_ge(x_lo, base + p + 1)
                    product(free(i, ("k", p)), WK, p, k_mm)
                    product(free(i, ("v", p)), WV, p, v_mm)
                    product(free(i, ("q", p)), WQ, p, q_mm)
                fold_bias(0)
                attn_out(0)
                attn_out(1)
                fold_bias(1)
                attn_out(2)
                attn_out(3)
                for p in range(PAIRS):
                    centered(base, i, 0, p)
                    stats(0, p)
                rstd(0, 0)
                rstd(0, 1)
                up(0)
                rstd(0, 2)
                rstd(0, 3)
                up(1)
                down(0)
                up(2)
                down(1)
                centered(base, i, 1, 0)
                stats(1, 0)
                up(3)
                centered(base, i, 1, 1)
                stats(1, 1)
                down(2)
                rstd(1, 0)
                rstd(1, 1)
                down(3)
                for p in (2, 3):
                    centered(base, i, 1, p)
                    stats(1, p)
                rstd(1, 2)
                rstd(1, 3)

            base = LAYERS * 2 * PAIRS
            calls = LAYERS * 2 * BATCHES
            for p in range(PAIRS):
                centered(base, LAYERS, 0, p, last=True)
                variances(base, (calls + p // PAIRS_PER_BATCH - 1) * RSQRT_STEPS + 1, 0, p)
            for p in range(PAIRS):
                spread(free(LAYERS, ("r0", p), True), p, calls + p // PAIRS_PER_BATCH, r_mm)
            for p in range(PAIRS):
                pe.wait_ge(x_lo, base + PAIRS + p + 1)
                for j in range(FT):
                    for dst, at in halves(free(LAYERS, ("h", p, j), True)):
                        t = slice(p * PAIR + at, p * PAIR + at + BANK)
                        pe.matmul(dst, tfc[:, j * P:(j + 1) * P], xh[:, t], start=True, stop=False)
                        mm = pe.matmul(dst, tfc[:, j * P:(j + 1) * P], xl[:, t], start=False, stop=True)
                    mm.then_inc(h_mm, 1)
                slot = free(LAYERS, ("f", p), True)
                pe.wait_ge(h_ready, LAYERS * PAIRS * FT + (p + 1) * FT)
                for dst, at in halves(slot):
                    for j in range(FT):
                        mm = pe.matmul(dst, pw[:, j * P:(j + 1) * P], h[:, p % 2, j * PAIR + at:j * PAIR + at + BANK],
                                       start=(j == 0), stop=(j == FT - 1))
                mm.then_inc(f_mm, 1)
                first, last = p % PAIRS_PER_BATCH == 0, p % PAIRS_PER_BATCH == PAIRS_PER_BATCH - 1
                pe.wait_ge(g_part, (p + 1) * (FT - 1))
                pe.wait_ge(s_sum, (p + 1) * (FT - 1))
                if first and p > 0:
                    pe.wait_ge(rsqrt, (calls + BATCHES + p // PAIRS_PER_BATCH - 1) * RSQRT_STEPS + 1)
                for bank, src in ((stat, kw), (small, a)):
                    for r in range(ROWS_PER_PAIR):
                        row = (p % PAIRS_PER_BATCH) * ROWS_PER_PAIR + r
                        mm = pe.matmul(bank[0:ROWS, 0:ROW], slide_ff[:, ROWS - 1 - row:2 * ROWS - 1 - row],
                                       src[:, p % 2, r * ROW:(r + 1) * ROW], start=first and r == 0,
                                       stop=last and r == ROWS_PER_PAIR - 1)
                    mm.then_inc(st_mm, 1)
            for p in range(PAIRS):
                spread(free(LAYERS, ("rf", p), True), p, calls + BATCHES + p // PAIRS_PER_BATCH, rf_mm)
            for p in range(PAIRS):
                centered(base, LAYERS, 1, p, last=True)
                variances(base, (calls + 2 * BATCHES + p // PAIRS_PER_BATCH - 1) * RSQRT_STEPS + 1, 1, p)
            for p in range(PAIRS):
                spread(free(LAYERS, ("r1", p), True), p, calls + 2 * BATCHES + p // PAIRS_PER_BATCH, r_mm)


def kernel(**inputs):
    import numpy as np
    import concourse.bacc as bacc
    from concourse.bass_utils import run_bass_kernel_spmd

    g = {n: np.asarray(v) for n, v in inputs.items()}
    at = lambda n: g["L0_attn_" + n]
    hidden_tiles = lambda w: w.reshape(w.shape[:-2] + (FT, P, w.shape[-1])).swapaxes(-3, -2).reshape(
        w.shape[:-2] + (P, FT * w.shape[-1]))
    vectors = [at(n)[:, :, None] for n in ("bq", "bk", "bv", "bo", "ln1_s", "ln1_b", "b2", "ln2_s", "ln2_b")]
    vectors.append(at("b1").reshape(LAYERS, FT, P).swapaxes(1, 2))
    layers = np.concatenate([at("Wq"), at("Wk"), at("Wv"), at("Wo"), at("W1"), hidden_tiles(at("W2"))] + vectors, axis=2)
    arrays = {
        "x_t": at("x").reshape(TOKENS, P).T,
        "layers": layers,
        "fc_t": g["L0_ffn_W_fc"].T,
        "proj_t": hidden_tiles(g["L0_ffn_W_proj"].T),
        "ffn_ln": np.concatenate([g["L0_ffn_ln_w"].reshape(FT, P).T, g["L0_ffn_ln_b"].reshape(FT, P).T], axis=1),
    }
    arrays = {n: np.ascontiguousarray(v) for n, v in arrays.items()}
    nc = bacc.Bacc("TRN2", target_bir_lowering=False, num_devices=1)
    args = [nc.dram_tensor(n, v.shape, mybir.dt.from_np(v.dtype), kind="ExternalInput").ap() for n, v in arrays.items()]
    out = nc.dram_tensor("out_t", (P, TOKENS), F32, kind="ExternalOutput").ap()
    build(nc, *args, out)
    r = run_bass_kernel_spmd(nc, [arrays], core_ids=[0])
    return np.ascontiguousarray(r.results[0]["out_t"].T).reshape(BATCHES, SEQ, P)
```

```python
from contextlib import ExitStack

import concourse.bass as bass
from concourse import mybir

P = 128
LAYERS = 4
BATCHES = 2
SEQ = 2048
TOKENS = BATCHES * SEQ
BANK = 512
PAIR = 2 * BANK
PAIRS = TOKENS // PAIR
PAIRS_PER_BATCH = PAIRS // BATCHES
FF = 512
FT = FF // P
ROW = 128
ROWS_PER_PAIR = PAIR // ROW
ROWS = PAIRS_PER_BATCH * ROWS_PER_PAIR
STEPS = LAYERS * BATCHES
LOW = 32
ZEPS = 1e-6
BLOCK_EPS = 1e-6
OUTER_EPS = 1e-5

F32 = mybir.dt.float32
F32R = mybir.dt.float32r
I32 = mybir.dt.int32
ALU = mybir.AluOpType
ACT = mybir.ActivationFunctionType
AX = mybir.AxisListType

WQ, WK, WV, WO, W1, W2 = 0, P, 2 * P, 3 * P, 4 * P, 4 * P + FF
PAR = W2 + FF
BQ, BK, BV, BO, LN1S, LN1B = range(6)
B2, LN2S, LN2B = range(3)
NATT, NOUT = 6, 3
LAYER_COLS = PAR + NATT + NOUT + FT
QKV = 3 * P

NEWTON_ROUNDS = 3
RSQRT_STEPS = 3 + 3 * NEWTON_ROUNDS
FOLD_STEPS = 7

RING = 4
ORDER = [("k", 0), ("v", 0), ("q", 0), ("k", 1), ("v", 1), ("q", 1), ("f", 0), ("f", 1), ("fold", 0), ("o", 0),
         ("o", 1), ("c2", 0), ("c2", 1), ("v2", 0), ("c1", 0), ("c1", 1), ("v1", 0), ("v1", 1), ("r1", 0),
         ("h", 0, 0), ("h", 0, 1), ("r1", 1), ("h", 0, 2), ("h", 0, 3), ("h", 1, 0), ("r2", 0), ("h", 1, 1),
         ("r2", 1), ("h", 1, 2), ("h", 1, 3), None, None]
assert len(ORDER) % RING == 0
OF_STEP_BEFORE = ("f", "c2", "v2", "r2")

LAST = [("cx", 0), ("cx", 1), ("vx", 0), ("cx", 2), ("cx", 3), ("vx", 1), ("rx", 0), ("rx", 1)]
LAST += [("h", 0, j) for j in range(FT)] + [("rx", 2), ("rx", 3)]
LAST += [("h", 1, j) for j in range(FT)] + [("f", 0), ("g", 0)]
LAST += [("h", 2, j) for j in range(FT)] + [("f", 1), ("g", 1), ("rf", 0)]
LAST += [("h", 3, j) for j in range(FT)] + [("f", 2), ("g", 2), ("rf", 1), ("cz", 0)]
LAST += [("f", 3), ("g", 3), ("rf", 2), ("cz", 1), ("vz", 0), ("rf", 3), ("rz", 0), ("rz", 1)]
LAST += [("cz", 2), ("cz", 3), ("vz", 1), ("rz", 2), ("rz", 3)]


def build(nc, x_in, layers_in, fc_in, proj_in, ffn_ln_in, out):
    with ExitStack() as ctx:
        def sb(name, shape, dt=F32):
            return ctx.enter_context(nc.sbuf_tensor(name, shape, dt))

        def sem(name):
            return ctx.enter_context(nc.semaphore(name))

        x = sb("x", [P, TOKENS])
        xh = sb("xh", [P, TOKENS], F32R)
        xl = sb("xl", [P, TOKENS], F32R)
        y = sb("y", [P, TOKENS])
        s = y
        yc = sb("yc", [P, TOKENS])
        h = sb("h", [P, 2, FT * PAIR])
        sq1 = sb("sq1", [P, 2, PAIR])
        sq2 = sb("sq2", [P, 2, PAIR])
        a1 = sb("a1", [P, 2, PAIR])
        a2 = sb("a2", [P, 2, PAIR])
        kw = sb("kw", [P, 2, PAIR])
        qw = sb("qw", [P, 2, PAIR])
        kk = sb("kk", [P, PAIR])
        raw = sb("raw", [P, LAYER_COLS])
        wh = sb("wh", [P, QKV + FF], F32R)
        wl = sb("wl", [P, QKV + FF], F32R)
        w2 = sb("w2", [P, FF])
        wo = sb("wo", [P, P])
        wo_kv = sb("wo_kv", [P, P])
        att = sb("att", [P, NATT])
        outp = sb("outp", [P, NOUT])
        b1 = sb("b1", [P, FT])
        bk1 = sb("bk1", [P, 2])
        bq1 = sb("bq1", [P, 1])
        ksum = sb("ksum", [P, PAIRS_PER_BATCH])
        kvsum = sb("kvsum", [P, PAIRS_PER_BATCH])
        fold = sb("fold", [P, FOLD_STEPS])
        bias_o = sb("bias_o", [P, 1])
        vv = sb("vv", [ROWS, ROW])
        ti = sb("ti", [ROWS, ROW], I32)
        tf = sb("tf", [ROWS, ROW])
        ry = sb("ry", [ROWS, ROW])
        mu = sb("mu", [ROWS, ROW])
        rr1 = sb("rr1", [LOW + ROWS_PER_PAIR, 2, ROW], F32R)
        rr2 = sb("rr2", [LOW + ROWS, ROW], F32R)
        rr3 = sb("rr3", [LOW + ROWS, ROW], F32R)
        center = sb("center", [P, P])
        slide = sb("slide", [P, 2 * ROWS - 1])
        slide_ff = sb("slide_ff", [P, 2 * ROWS - 1])
        ones = sb("ones", [P, P])
        ones_ff = sb("ones_ff", [P, P])
        pick = sb("pick", [LOW + ROWS, ROWS, P], F32R)
        fc = h[:, 0, 0:FF]
        proj = h[:, 0, FF:2 * FF]
        tern = h[:, 0, 2 * FF:3 * FF]
        ffn_norm = sb("ffn_norm", [P, 2 * FT])
        tfc = sb("tfc", [P, FF], F32R)
        pw = sb("pw", [P, FF])
        gam = sb("gam", [P, 2, 4])
        cb = sb("cb", [P, 1])

        tile = [ctx.enter_context(nc.psum_tensor(f"tile{n}", [P, PAIR], F32)) for n in range(RING)]

        x_loaded, w_in, ffn_in, x_again, stored = (sem(n) for n in ("x_loaded", "w_in", "ffn_in", "x_again", "stored"))
        const_ready, zero_ready, g_part = (sem(n) for n in ("const_ready", "zero_ready", "g_part"))
        k_mm, v_mm, q_mm, fold_mm, o_mm, h_mm, f_mm, gam_mm, cb_mm, pw_mm, rf_mm, g_mm = (
            sem(n) for n in ("k_mm", "v_mm", "q_mm", "fold_mm", "o_mm", "h_mm", "f_mm", "gam_mm", "cb_mm", "pw_mm",
                             "rf_mm", "g_mm"))
        k_neg, k_exp, q_exp, s_ln, s_ready, o_once, o_ready, f_ready, h_ready, g_sq, p_out = (
            sem(n) for n in ("k_neg", "k_exp", "q_exp", "s_ln", "s_ready", "o_once", "o_ready", "f_ready", "h_ready",
                             "g_sq", "p_out"))
        att_ready, w_hi, w_lo, w1_hi, w1_lo, w2_ready, b_ready = (
            sem(n) for n in ("att_ready", "w_hi", "w_lo", "w1_hi", "w1_lo", "w2_ready", "b_ready"))
        k_round, k_ready, kv_ready, q_neg, q_round, q_max, folded, bias_ready = (
            sem(n) for n in ("k_round", "k_ready", "kv_ready", "q_neg", "q_round", "q_max", "folded", "bias_ready"))
        tern_step, gam_step, s_sum, moment, y_step = (
            sem(n) for n in ("tern_step", "gam_step", "s_sum", "moment", "y_step"))
        y_ready, c_mm, yc_ready, sq_ready, var_mm, rsqrt, r_ready, r_mm, x_norm, x_new, x_hi, x_lo = (
            {n: sem(f"{name}_{n}") for n in names} for name, names in (
                ("y_ready", "12xz"), ("c_mm", "12xz"), ("yc_ready", "12xz"), ("sq_ready", "12xz"), ("var_mm", "12xz"),
                ("rsqrt", "12xzg"), ("r_ready", "12xzg"), ("r_mm", "12xz"), ("x_norm", "12xz"), ("x_new", "12"),
                ("x_hi", "12x"), ("x_lo", "12x")))
        squares_of = {"1": sq1, "2": sq2, "x": sq1, "z": sq2}

        def cols(n, p):
            return slice(n * SEQ + p * PAIR, n * SEQ + (p + 1) * PAIR)

        def ge(eng, sem, value):
            if not isinstance(value, int) or value > 0:
                eng.wait_ge(sem, value)

        def slot_of(key):
            return ORDER.index(key) % RING

        def last_slot_of(key):
            return LAST.index(key) % RING

        def reader(t, key):
            kind, p = key[0], key[1]
            of_t = 2 * t + p + 1
            of_b = 2 * (t - 1) + p + 1
            return {
                "k": (k_ready, of_t), "v": (kv_ready, of_t), "q": (q_max, of_t), "o": (o_once, of_t),
                "fold": (bias_ready, t + 1), "h": (h_ready, 2 * FT * t + p * FT + key[-1] + 1),
                "c1": (sq_ready["1"], of_t), "v1": (rsqrt["1"], (of_t - 1) * RSQRT_STEPS + 1),
                "r1": (x_norm["1"], of_t), "f": (f_ready, of_b), "c2": (sq_ready["2"], of_b),
                "v2": (rsqrt["2"], (t - 1) * RSQRT_STEPS + 1), "r2": (x_norm["2"], of_b),
            }[kind]

        def last_reader(key):
            kind, p = key[0], key[1]
            steps = RSQRT_STEPS
            return {
                "h": (h_ready, 2 * FT * STEPS + p * FT + key[-1] + 1), "f": (p_out, p + 1), "rf": (y_step, p + 1),
                "g": (moment, 3 * p + 2),
                "cx": (sq_ready["x"], p + 1), "vx": (rsqrt["x"], p * steps + 1), "rx": (x_norm["x"], p + 1),
                "cz": (sq_ready["z"], p + 1), "vz": (rsqrt["z"], p * steps + 1), "rz": (x_norm["z"], p + 1),
            }[kind]

        block = ctx.enter_context(nc.Block())

        @block.sync
        def _(sp):
            sp.dma_start(raw[:, :], layers_in[0]).then_inc(w_in, 16)
            for p in range(PAIRS):
                sp.dma_start(x[:, p * PAIR:(p + 1) * PAIR], x_in[:, p * PAIR:(p + 1) * PAIR]).then_inc(x_loaded, 16)
            sp.dma_start(fc, fc_in).then_inc(ffn_in, 16)
            sp.dma_start(proj, proj_in).then_inc(ffn_in, 16)
            sp.dma_start(ffn_norm[:, :], ffn_ln_in).then_inc(ffn_in, 16)
            with sp.Fori(1, LAYERS) as i:
                sp.wait_ge(w2_ready, 2 * i)
                sp.dma_start(raw[:, :], layers_in[bass.ds(i, 1), :, :].rearrange("a p n -> (a p) n")).then_inc(w_in, 16)
            for n in range(BATCHES):
                sp.wait_ge(c_mm["2"], 2 * (STEPS - BATCHES + n) + 2)
                sp.dma_start(y[:, n * SEQ:(n + 1) * SEQ], x_in[:, n * SEQ:(n + 1) * SEQ]).then_inc(x_again, 16)
            for p in range(PAIRS):
                sp.wait_ge(x_norm["z"], p + 1)
                sp.dma_start(out[:, p * PAIR:(p + 1) * PAIR], x[:, p * PAIR:(p + 1) * PAIR]).then_inc(stored, 16)
            sp.wait_ge(stored, 16 * PAIRS)

        @block.gpsimd
        def _(pool):
            pool.memset(center[:, :], -1.0 / P).then_inc(zero_ready, 1)
            pool.memset(slide[:, :], 0.0).then_inc(zero_ready, 1)
            pool.memset(slide_ff[:, :], 0.0).then_inc(zero_ready, 1)
            pool.memset(pick[:, :, :].bitcast(F32), 0.0).then_inc(zero_ready, 1)
            pool.memset(rr1[:, :, :].bitcast(F32), 0.0).then_inc(const_ready, 1)
            pool.memset(rr2[:, :].bitcast(F32), 0.0).then_inc(const_ready, 1)
            pool.memset(rr3[:, :].bitcast(F32), 0.0).then_inc(const_ready, 1)
            pool.memset(ones[:, :], 1.0).then_inc(const_ready, 1)
            pool.memset(ones_ff[:, :], 1.0 / FF).then_inc(const_ready, 1)
            pool.wait_ge(zero_ready, 4)
            pool.affine_select(out=center[:, :], in_=center[:, :], compare_op=ALU.not_equal, fill=1.0 - 1.0 / P,
                               base=0, pattern=[[-1, P]], channel_multiplier=1).then_inc(const_ready, 1)
            pool.memset(slide[:, ROWS - 1:ROWS], 1.0 / P).then_inc(const_ready, 1)
            pool.memset(slide_ff[:, ROWS - 1:ROWS], 1.0 / FF).then_inc(const_ready, 1)
            pool.affine_select(out=pick[:, :, :], in_=pick[:, :, :], compare_op=ALU.not_equal, fill=1.0,
                               base=0, pattern=[[-1, ROWS], [0, P]], channel_multiplier=1).then_inc(zero_ready, 1)
            pool.wait_ge(zero_ready, 5)
            pool.affine_select(out=pick[:, :, :], in_=pick[:, :, :], compare_op=ALU.not_equal, fill=1.0,
                               base=-LOW, pattern=[[-1, ROWS], [0, P]], channel_multiplier=1).then_inc(const_ready, 1)

            def low_parts(n, t):
                for p in range(PAIRS_PER_BATCH):
                    m = PAIRS + 2 * (t - 1) + p
                    pool.wait_ge(x_hi["2"], m + 1)
                    pool.tensor_tensor(xl[:, cols(n, p)], x[:, cols(n, p)], xh[:, cols(n, p)].bitcast(F32),
                                       ALU.subtract).then_inc(x_lo["2"], 1)

            with pool.Fori(0, LAYERS - 1) as i:
                low_parts(0, 2 * i + 1)
                low_parts(1, 2 * i + 2)
            for p in range(PAIRS):
                pool.wait_ge(h_ready, 2 * FT * STEPS + p * FT + 2)
                if p >= 2:
                    pool.wait_ge(g_mm, 2 * (p - 1))
                pool.tensor_tensor(kw[:, p % 2, :], h[:, p % 2, 0:PAIR], h[:, p % 2, PAIR:2 * PAIR],
                                   ALU.add).then_inc(g_part, 1)
                for j in range(2, FT):
                    pool.wait_ge(h_ready, 2 * FT * STEPS + p * FT + j + 1)
                    pool.wait_ge(g_part, p * (FT - 1) + j - 1)
                    pool.tensor_tensor(kw[:, p % 2, :], kw[:, p % 2, :], h[:, p % 2, j * PAIR:(j + 1) * PAIR],
                                       ALU.add).then_inc(g_part, 1)

        @block.scalar
        def _(act):
            def squares(k, slot, n, p, done, reuse=None):
                act.wait_ge(c_mm[k], done + 1)
                act.activation(yc[:, cols(n, p)], tile[slot][:, :], ACT.Copy).then_inc(yc_ready[k], 1)
                if reuse is not None:
                    act.wait_ge(var_mm[k], reuse)
                act.activation(squares_of[k][:, p, :], tile[slot][:, :], ACT.Square).then_inc(sq_ready[k], 1)

            def step(t, n, layer, attend=True, left=True):
                def exps(p):
                    m = 2 * t + p
                    act.wait_ge(k_mm, m + 1)
                    act.activation(kw[:, p, :], tile[slot_of(("k", p))][:, :], ACT.Relu, bias=bk1[:, 0:1],
                                   scale=-1.0).then_inc(k_neg, 1)
                    act.wait_ge(k_neg, m + 1)
                    act.activation(kw[:, p, :], kw[:, p, :], ACT.Exp, scale=-1.0).then_inc(k_exp, 1)
                    act.wait_ge(q_neg, m + 1)
                    act.activation(qw[:, p, :], qw[:, p, :], ACT.Exp).then_inc(q_exp, 1)

                def shares(p):
                    act.wait_ge(folded, t * FOLD_STEPS + 3)
                    act.wait_ge(q_max, 2 * t + p + 1)
                    act.activation(s[:, cols(n, p)], s[:, cols(n, p)], ACT.Ln, bias=1.0,
                                   scale=fold[:, 2:3]).then_inc(s_ln, 1)

                def shares_out(p):
                    act.wait_ge(s_ln, 2 * t + p + 1)
                    act.activation(s[:, cols(n, p)], s[:, cols(n, p)], ACT.Exp, scale=-1.0).then_inc(s_ready, 1)

                if attend:
                    act.preload_act_table_set("natural_log_exp_and_others")
                    act.wait_ge(b_ready, 3 * (layer + 1))
                    exps(0)
                    exps(1)
                    shares(0)
                    shares(1)
                    shares_out(0)
                    shares_out(1)
                if left:
                    for p in range(2):
                        act.wait_ge(f_mm, 2 * (t - 1) + p + 1)
                        act.activation(a2[:, p, :], tile[slot_of(("f", p))][:, :], ACT.Gelu_apprx_tanh,
                                       bias=outp[:, B2:B2 + 1]).then_inc(f_ready, 1)
                if attend:
                    act.wait_ge(bias_ready, t + 1)
                    for p in range(2):
                        act.wait_ge(o_mm, 2 * t + p + 1)
                        act.activation(a1[:, p, :], tile[slot_of(("o", p))][:, :], ACT.Gelu_apprx_tanh,
                                       bias=bias_o[:, 0:1]).then_inc(o_once, 1)
                    for p in range(2):
                        act.wait_ge(o_once, 2 * t + p + 1)
                        act.activation(a1[:, p, :], a1[:, p, :], ACT.Gelu_apprx_tanh).then_inc(o_ready, 1)
                if left:
                    for p in range(2):
                        squares("2", slot_of(("c2", p)), 1 - n, p, 2 * (t - 1) + p)
                if attend:
                    for p in range(2):
                        squares("1", slot_of(("c1", p)), n, p, 2 * t + p)
                    for p in range(2):
                        for j in range(FT):
                            act.wait_ge(h_mm, 2 * FT * t + p * FT + j + 1)
                            act.activation(h[:, p, j * PAIR:(j + 1) * PAIR], tile[slot_of(("h", p, j))][:, :],
                                           ACT.Gelu_apprx_tanh, bias=b1[:, j:j + 1]).then_inc(h_ready, 1)

            act.wait_ge(const_ready, 9)
            step(0, 0, 0, left=False)
            with act.Fori(0, LAYERS - 1) as i:
                step(2 * i + 1, 1, i)
                step(2 * i + 2, 0, i + 1)
            step(STEPS - 1, 1, LAYERS - 1)
            step(STEPS, 0, LAYERS, attend=False)

            def last_squares(k, p):
                squares(k, last_slot_of((f"c{k}", p)), p // 2, p % 2, p, (p // 2) if p >= 2 else None)

            def last_hidden(p):
                for j in range(FT):
                    act.wait_ge(h_mm, 2 * FT * STEPS + p * FT + j + 1)
                    if p >= 2 and j == 0:
                        act.wait_ge(f_mm, 2 * STEPS + p - 1)
                    act.activation(h[:, p % 2, j * PAIR:(j + 1) * PAIR], tile[last_slot_of(("h", p, j))][:, :],
                                   ACT.Gelu).then_inc(h_ready, 1)
                for j in range(FT):
                    act.wait_ge(h_ready, 2 * FT * STEPS + p * FT + j + 1)
                    if j == 0:
                        if p >= 2:
                            act.wait_ge(g_mm, 2 * (p - 1))
                        act.activation(a1[:, p % 2, :], h[:, p % 2, 0:PAIR], ACT.Square).then_inc(g_sq, 1)
                        continue
                    done = p * (FT - 1) + j - 2
                    if done > 0:
                        act.wait_ge(s_sum, done)
                    act.activation(qw[:, (p * (FT - 1) + j - 1) % 2, :], h[:, p % 2, j * PAIR:(j + 1) * PAIR],
                                   ACT.Square).then_inc(g_sq, 1)

            def projected(p):
                act.wait_ge(f_mm, 2 * STEPS + p + 1)
                act.activation(yc[:, cols(p // 2, p % 2)], tile[last_slot_of(("f", p))][:, :], ACT.Copy).then_inc(p_out, 1)

            for p in range(PAIRS):
                last_squares("x", p)
            last_hidden(0)
            last_hidden(1)
            projected(0)
            last_hidden(2)
            projected(1)
            last_hidden(3)
            projected(2)
            projected(3)
            for p in range(PAIRS):
                last_squares("z", p)

        @block.vector
        def _(dve):
            def rsqrt_of(k, call, src, rows, high, low, eps, variance=None):
                base = call * RSQRT_STEPS
                v, i, f, r = (z[0:rows, :] for z in (vv, ti, tf, ry))
                if variance is None:
                    dve.tensor_scalar(v, src, eps, None, ALU.add).then_inc(rsqrt[k], 1)
                else:
                    variance(rsqrt[k])
                dve.wait_ge(rsqrt[k], base + 1)
                dve.tensor_scalar(i, v.bitcast(I32), 1, None, ALU.logical_shift_right).then_inc(rsqrt[k], 1)
                dve.wait_ge(rsqrt[k], base + 2)
                dve.tensor_scalar(r.bitcast(I32), i, -1.0, float(0x5F3759DF), ALU.mult, ALU.add).then_inc(rsqrt[k], 1)
                for n in range(NEWTON_ROUNDS):
                    dve.wait_ge(rsqrt[k], base + 3 + 3 * n)
                    dve.tensor_tensor(f, r, r, ALU.mult).then_inc(rsqrt[k], 1)
                    dve.wait_ge(rsqrt[k], base + 4 + 3 * n)
                    dve.scalar_tensor_tensor(f, f, -0.5, v, ALU.mult, ALU.mult).then_inc(rsqrt[k], 1)
                    dve.wait_ge(rsqrt[k], base + 5 + 3 * n)
                    dve.scalar_tensor_tensor(r, f, 1.5, r, ALU.add, ALU.mult).then_inc(rsqrt[k], 1)
                dve.wait_ge(rsqrt[k], base + RSQRT_STEPS)
                dve.tensor_copy(high, r).then_inc(r_ready[k], 1)
                dve.wait_ge(r_ready[k], 2 * call + 1)
                dve.tensor_tensor(low, r, high.bitcast(F32), ALU.subtract).then_inc(r_ready[k], 1)

            def normed(k, slot, n, p, done, scale, shift):
                c = cols(n, p)
                dve.wait_ge(r_mm[k], done + 1)
                dve.wait_ge(yc_ready[k], done + 1)
                dve.scalar_tensor_tensor(x[:, c], yc[:, c], scale, tile[slot][:, :], ALU.mult,
                                         ALU.mult).then_inc(x_norm[k], 1)
                dve.wait_ge(x_norm[k], done + 1)
                if shift is not None:
                    dve.tensor_scalar(x[:, c], x[:, c], shift, None, ALU.add).then_inc(x_new[k], 1)
                    dve.wait_ge(x_new[k], done + 1)

            def split_high(k, n, p):
                dve.tensor_copy(xh[:, cols(n, p)], x[:, cols(n, p)]).then_inc(x_hi[k], 1)

            def split_low(k, n, p, done):
                dve.wait_ge(x_hi[k], done + 1)
                dve.tensor_tensor(xl[:, cols(n, p)], x[:, cols(n, p)], xh[:, cols(n, p)].bitcast(F32),
                                  ALU.subtract).then_inc(x_lo[k], 1)

            def take_attention(layer):
                dve.wait_ge(w_in, 16 * (layer + 1))
                dve.tensor_copy(wh[:, 0:QKV], raw[:, 0:QKV]).then_inc(w_hi, 1)
                dve.tensor_copy(att[:, :], raw[:, PAR:PAR + NATT]).then_inc(att_ready, 1)
                dve.tensor_copy(wo[:, :], raw[:, WO:WO + P]).then_inc(att_ready, 1)
                dve.wait_ge(w_hi, layer + 1)
                dve.tensor_tensor(wl[:, 0:QKV], raw[:, 0:QKV], wh[:, 0:QKV].bitcast(F32), ALU.subtract).then_inc(w_lo, 1)
                dve.wait_ge(att_ready, 2 * layer + 2)
                dve.tensor_scalar(bk1[:, 0:1], att[:, BK:BK + 1], -1.0, None, ALU.mult).then_inc(b_ready, 1)
                dve.tensor_scalar(bk1[:, 1:2], att[:, BK:BK + 1], 1.0, None, ALU.add).then_inc(b_ready, 1)
                dve.tensor_scalar(bq1[:, :], att[:, BQ:BQ + 1], 1.0, None, ALU.add).then_inc(b_ready, 1)
                dve.wait_ge(b_ready, 3 * (layer + 1))

            def take_up(layer):
                dve.tensor_copy(wh[:, QKV:], raw[:, W1:W1 + FF]).then_inc(w1_hi, 1)
                dve.wait_ge(w1_hi, layer + 1)
                dve.tensor_tensor(wl[:, QKV:], raw[:, W1:W1 + FF], wh[:, QKV:].bitcast(F32), ALU.subtract).then_inc(w1_lo, 1)
                dve.tensor_copy(b1[:, :], raw[:, PAR + NATT + NOUT:LAYER_COLS]).then_inc(w1_lo, 1)

            def take_down(layer):
                dve.tensor_copy(w2[:, :], raw[:, W2:W2 + FF]).then_inc(w2_ready, 1)
                dve.tensor_copy(outp[:, :], raw[:, PAR + NATT:PAR + NATT + NOUT]).then_inc(w2_ready, 1)
                dve.wait_ge(w2_ready, 2 * (layer + 1))

            def step(t, n, layer, attend=True, left=True):
                def sums(p):
                    m = 2 * t + p
                    k_tile, v_tile, q_tile = (tile[slot_of((z, p))] for z in "kvq")
                    dve.wait_ge(k_exp, m + 1)
                    dve.tensor_scalar(kw[:, p, :], kw[:, p, :], -1.0, 1.0, ALU.add, ALU.add).then_inc(k_round, 1)
                    dve.wait_ge(k_round, m + 1)
                    if p > 0:
                        dve.wait_ge(kv_ready, m)
                    dve.scalar_tensor_tensor(kk[:, :], k_tile[:, :], bk1[:, 1:2], kw[:, p, :], ALU.add,
                                             ALU.max, accum_out=ksum[:, p:p + 1]).then_inc(k_ready, 1)
                    dve.wait_ge(q_mm, m + 1)
                    dve.tensor_scalar(qw[:, p, :], q_tile[:, :], att[:, BQ:BQ + 1], 0.0, ALU.add,
                                      ALU.min).then_inc(q_neg, 1)
                    dve.wait_ge(k_ready, m + 1)
                    dve.wait_ge(v_mm, m + 1)
                    dve.scalar_tensor_tensor(kk[:, :], v_tile[:, :], att[:, BV:BV + 1], kk[:, :], ALU.add,
                                             ALU.mult, accum_out=kvsum[:, p:p + 1]).then_inc(kv_ready, 1)
                    dve.wait_ge(q_exp, m + 1)
                    dve.tensor_scalar(qw[:, p, :], qw[:, p, :], -1.0, 1.0, ALU.add, ALU.add).then_inc(q_round, 1)
                    dve.wait_ge(q_round, m + 1)
                    dve.scalar_tensor_tensor(s[:, cols(n, p)], q_tile[:, :], bq1[:, 0:1], qw[:, p, :], ALU.add,
                                             ALU.max).then_inc(q_max, 1)

                def fold_kv():
                    base = t * FOLD_STEPS
                    col = [fold[:, c:c + 1] for c in range(FOLD_STEPS)]
                    dve.wait_ge(kv_ready, 2 * t + 2)
                    dve.tensor_tensor(col[0], ksum[:, 0:1], ksum[:, 1:2], ALU.add).then_inc(folded, 1)
                    dve.tensor_tensor(col[1], kvsum[:, 0:1], kvsum[:, 1:2], ALU.add).then_inc(folded, 1)
                    dve.wait_ge(folded, base + 2)
                    dve.tensor_scalar(col[2], col[0], 1.0 / ZEPS, None, ALU.mult).then_inc(folded, 1)
                    dve.tensor_scalar(col[3], col[0], 2.0 ** -30, None, ALU.max).then_inc(folded, 1)
                    dve.wait_ge(folded, base + 4)
                    dve.reciprocal(col[4], col[3]).then_inc(folded, 1)
                    dve.wait_ge(folded, base + 5)
                    dve.tensor_tensor(col[5], col[1], col[4], ALU.mult).then_inc(folded, 1)
                    dve.wait_ge(folded, base + 6)
                    dve.tensor_scalar(wo_kv[:, :], wo[:, :], col[5], -1.0, ALU.mult, ALU.mult).then_inc(folded, 1)
                    dve.wait_ge(fold_mm, t + 1)
                    dve.tensor_tensor(bias_o[:, :], tile[slot_of(("fold", 0))][:, 0:1], att[:, BO:BO + 1],
                                      ALU.add).then_inc(bias_ready, 1)

                b = 1 - n
                if attend:
                    sums(0)
                    sums(1)
                    fold_kv()
                    if n == 0:
                        take_up(layer)
                if left:
                    for p in range(2):
                        dve.wait_ge(f_ready, 2 * (t - 1) + p + 1)
                        dve.tensor_tensor(y[:, cols(b, p)], a2[:, p, :], x[:, cols(b, p)], ALU.add).then_inc(y_ready["2"], 1)
                if attend:
                    for p in range(2):
                        dve.wait_ge(o_ready, 2 * t + p + 1)
                        dve.tensor_tensor(y[:, cols(n, p)], a1[:, p, :], x[:, cols(n, p)], ALU.add).then_inc(y_ready["1"], 1)
                if left:
                    dve.wait_ge(var_mm["2"], t)
                    rsqrt_of("2", t - 1, tile[slot_of(("v2", 0))][0:ROWS, 0:ROW], ROWS, rr2[0:ROWS, :],
                             rr2[LOW:LOW + ROWS, :], BLOCK_EPS)
                if attend:
                    for p in range(2):
                        m = 2 * t + p
                        dve.wait_ge(var_mm["1"], m + 1)
                        rsqrt_of("1", m, tile[slot_of(("v1", p))][0:ROWS_PER_PAIR, 0:ROW], ROWS_PER_PAIR,
                                 rr1[0:ROWS_PER_PAIR, p, :], rr1[LOW:LOW + ROWS_PER_PAIR, p, :], BLOCK_EPS)
                        normed("1", slot_of(("r1", p)), n, p, m, att[:, LN1S:LN1S + 1], att[:, LN1B:LN1B + 1])
                        split_high("1", n, p)
                        split_low("1", n, p, m)
                if left:
                    for p in range(2):
                        normed("2", slot_of(("r2", p)), b, p, 2 * (t - 1) + p, outp[:, LN2S:LN2S + 1], outp[:, LN2B:LN2B + 1])
                        split_high("2", b, p)
                if attend and n == 0:
                    take_down(layer)

            take_attention(0)
            for p in range(PAIRS):
                dve.wait_ge(x_loaded, 16 * PAIRS)
                split_high("2", p // 2, p % 2)
                split_low("2", p // 2, p % 2, p)

            dve.wait_ge(ffn_in, 48)
            for n, w in enumerate((fc, proj)):
                dve.tensor_reduce(gam[:, n, 0:1], w, AX.X, ALU.add, apply_absolute_value=True).then_inc(gam_step, 1)
            dve.wait_ge(gam_mm, 1)
            for n, (w, z) in enumerate(((fc, tfc), (proj, pw))):
                base = 5 * n
                dve.tensor_scalar(gam[:, n, 1:2], tile[0][:, n:n + 1], 1.0 / (P * FF), 1e-6, ALU.mult,
                                  ALU.add).then_inc(tern_step, 1)
                dve.wait_ge(tern_step, base + 1)
                dve.tensor_scalar(gam[:, n, 2:3], gam[:, n, 1:2], 0.5, None, ALU.mult).then_inc(tern_step, 1)
                dve.tensor_scalar(gam[:, n, 3:4], gam[:, n, 1:2], -0.5, None, ALU.mult).then_inc(tern_step, 1)
                dve.wait_ge(tern_step, base + 3)
                dve.tensor_scalar(tern, w, gam[:, n, 3:4], None, ALU.is_lt).then_inc(tern_step, 1)
                dve.wait_ge(tern_step, base + 4)
                dve.scalar_tensor_tensor(z[:, :], w, gam[:, n, 2:3], tern, ALU.is_gt, ALU.subtract).then_inc(tern_step, 1)
                dve.wait_ge(tern_step, base + 5)
            dve.wait_ge(cb_mm, 1)
            dve.tensor_copy(cb[:, :], tile[1][:, 0:1]).then_inc(gam_step, 1)
            for j in range(FT):
                dve.tensor_scalar(pw[:, j * P:(j + 1) * P], pw[:, j * P:(j + 1) * P], ffn_norm[:, j:j + 1], None,
                                  ALU.mult).then_inc(gam_step, 1)
            dve.wait_ge(gam_step, 3 + FT)
            dve.wait_ge(pw_mm, 1)
            for j in range(FT):
                dve.tensor_tensor(pw[:, j * P:(j + 1) * P], pw[:, j * P:(j + 1) * P], tile[2][:, 0:P],
                                  ALU.subtract).then_inc(gam_step, 1)

            step(0, 0, 0, left=False)
            with dve.Fori(0, LAYERS - 1) as i:
                step(2 * i + 1, 1, i)
                take_attention(i + 1)
                step(2 * i + 2, 0, i + 1)
            step(STEPS - 1, 1, LAYERS - 1)
            step(STEPS, 0, LAYERS, attend=False)

            def rsqrt_rows(k, b):
                dve.wait_ge(var_mm[k], b + 1)
                rr = (rr2, rr3)[b]
                rsqrt_of(k, b, tile[last_slot_of((f"v{k}", b))][0:ROWS, 0:ROW], ROWS, rr[0:ROWS, :],
                         rr[LOW:LOW + ROWS, :], OUTER_EPS)

            dve.wait_ge(x_again, 16 * BATCHES)
            for p in range(PAIRS):
                c = cols(p // 2, p % 2)
                dve.tensor_tensor(y[:, c], y[:, c], x[:, c], ALU.add).then_inc(y_ready["x"], 1)
            rsqrt_rows("x", 0)
            rsqrt_rows("x", 1)
            for p in range(PAIRS):
                normed("x", last_slot_of(("rx", p)), p // 2, p % 2, p, 1.0, None)
                split_high("x", p // 2, p % 2)
                split_low("x", p // 2, p % 2, p)

            def square_sum(p):
                for j in range(1, FT):
                    m = p * (FT - 1) + j - 1
                    dve.wait_ge(g_sq, p * FT + j + 1)
                    if m > 0:
                        dve.wait_ge(s_sum, m)
                    dve.tensor_tensor(a1[:, p % 2, :], a1[:, p % 2, :], qw[:, m % 2, :], ALU.add).then_inc(s_sum, 1)

            def hidden_rsqrt(p):
                dve.wait_ge(g_mm, 2 * (p + 1))
                g = tile[last_slot_of(("g", p))][0:ROWS_PER_PAIR, :]
                m, v = mu[0:ROWS_PER_PAIR, :], vv[0:ROWS_PER_PAIR, :]

                def variance(done):
                    dve.tensor_copy(m, g[:, 0:ROW]).then_inc(moment, 1)
                    dve.tensor_scalar(v, g[:, BANK:BANK + ROW], OUTER_EPS, None, ALU.add).then_inc(moment, 1)
                    dve.wait_ge(moment, 3 * p + 2)
                    dve.tensor_tensor(m, m, m, ALU.mult).then_inc(moment, 1)
                    dve.wait_ge(moment, 3 * p + 3)
                    dve.tensor_tensor(v, v, m, ALU.subtract).then_inc(done, 1)

                rsqrt_of("g", p, None, ROWS_PER_PAIR, rr1[0:ROWS_PER_PAIR, p % 2, :],
                         rr1[LOW:LOW + ROWS_PER_PAIR, p % 2, :], OUTER_EPS, variance)

            def fed_forward(p):
                c = cols(p // 2, p % 2)
                dve.wait_ge(rf_mm, p + 1)
                dve.wait_ge(p_out, p + 1)
                dve.tensor_tensor(yc[:, c], yc[:, c], tile[last_slot_of(("rf", p))][:, :], ALU.mult).then_inc(y_step, 1)
                dve.wait_ge(y_step, p + 1)
                dve.scalar_tensor_tensor(y[:, c], yc[:, c], cb[:, 0:1], x[:, c], ALU.add, ALU.add).then_inc(y_ready["z"], 1)

            square_sum(0)
            square_sum(1)
            hidden_rsqrt(0)
            square_sum(2)
            fed_forward(0)
            hidden_rsqrt(1)
            square_sum(3)
            fed_forward(1)
            hidden_rsqrt(2)
            fed_forward(2)
            rsqrt_rows("z", 0)
            hidden_rsqrt(3)
            fed_forward(3)
            for p in range(PAIRS):
                if p == PAIRS_PER_BATCH:
                    rsqrt_rows("z", 1)
                normed("z", last_slot_of(("rz", p)), p // 2, p % 2, p, 1.0, None)

        @block.tensor
        def _(pe):
            def halves(slot):
                return [(tile[slot][:, c * BANK:(c + 1) * BANK], c * BANK) for c in range(PAIR // BANK)]

            def part(n, p, at):
                return slice(n * SEQ + p * PAIR + at, n * SEQ + p * PAIR + at + BANK)

            def centered(k, slot, n, p, ready):
                ge(pe, y_ready[k], ready)
                for dst, at in halves(slot):
                    mm = pe.matmul(dst, center[:, :], y[:, part(n, p, at)], start=True, stop=True)
                mm.then_inc(c_mm[k], 1)

            def mean_rows(dst, weights, rows, src, row0, first, last):
                for r in range(ROWS_PER_PAIR):
                    at = ROWS - 1 - row0 - r
                    mm = pe.matmul(dst, weights[:, at:at + rows], src[:, r * ROW:(r + 1) * ROW],
                                   start=first and r == 0, stop=last and r == ROWS_PER_PAIR - 1)
                return mm

            def spread(slot, rr, rows, row0):
                for r in range(ROWS_PER_PAIR):
                    mm = pe.matmul(tile[slot][:, r * ROW:(r + 1) * ROW], pick[0:LOW + rows, row0 + r, :], rr,
                                   start=True, stop=True)
                return mm

            def step(t, n, layer, attend=True, left=True):
                def absent(key):
                    return key is None or not (left if key[0] in OF_STEP_BEFORE else attend)

                def free(key):
                    at = ORDER.index(key) - RING
                    while absent(ORDER[at]) if at >= 0 else ORDER[at] is None:
                        at -= RING
                    earlier = ORDER[at]
                    if at < 0 and earlier[0] == "r2":
                        pe.wait_ge(x_hi["2"], 2 * t + earlier[1] + 1)
                    elif at < 0:
                        ge(pe, *reader(t - 1, earlier))
                    else:
                        ge(pe, *reader(t, earlier))
                    return slot_of(key)

                def product(slot, w0, p, done):
                    for dst, at in halves(slot):
                        c = part(n, p, at)
                        pe.matmul(dst, wh[:, w0:w0 + P], xh[:, c], start=True, stop=False)
                        pe.matmul(dst, wh[:, w0:w0 + P], xl[:, c], start=False, stop=False)
                        mm = pe.matmul(dst, wl[:, w0:w0 + P], xh[:, c], start=False, stop=True)
                    mm.then_inc(done, 1)

                def up(p, j):
                    if j == 0:
                        pe.wait_ge(w1_lo, 2 * layer + 2)
                        pe.wait_ge(x_lo["1"], 2 * t + p + 1)
                    product(free(("h", p, j)), QKV + j * P, p, h_mm)

                def first_rstd(p):
                    slot = free(("r1", p))
                    pe.wait_ge(r_ready["1"], 2 * (2 * t + p + 1))
                    spread(slot, rr1[:, p, :], ROWS_PER_PAIR, 0).then_inc(r_mm["1"], 1)

                def second_rstd(p):
                    if not left:
                        return
                    slot = free(("r2", p))
                    pe.wait_ge(r_ready["2"], 2 * t)
                    spread(slot, rr2[:, :], ROWS, p * ROWS_PER_PAIR).then_inc(r_mm["2"], 1)

                b = 1 - n
                if attend:
                    pe.wait_ge(w_lo, layer + 1)
                    for p in range(2):
                        pe.wait_ge(x_lo["2"], 2 * t + p + 1)
                        product(free(("k", p)), WK, p, k_mm)
                        product(free(("v", p)), WV, p, v_mm)
                        product(free(("q", p)), WQ, p, q_mm)
                if left:
                    pe.wait_ge(w2_ready, 2 * (layer if attend and n == 0 else layer + 1) if attend else 2 * LAYERS)
                    for p in range(2):
                        slot = free(("f", p))
                        pe.wait_ge(h_ready, 2 * FT * (t - 1) + (p + 1) * FT)
                        for dst, at in halves(slot):
                            for j in range(FT):
                                mm = pe.matmul(dst, w2[:, j * P:(j + 1) * P], h[:, p, j * PAIR + at:j * PAIR + at + BANK],
                                               start=(j == 0), stop=(j == FT - 1))
                        mm.then_inc(f_mm, 1)
                if attend:
                    slot = free(("fold", 0))
                    pe.wait_ge(folded, (t + 1) * FOLD_STEPS)
                    pe.matmul(tile[slot][:, 0:1], wo[:, :], fold[:, 5:6], start=True, stop=True).then_inc(fold_mm, 1)
                    for p in range(2):
                        slot = free(("o", p))
                        pe.wait_ge(s_ready, 2 * t + p + 1)
                        for dst, at in halves(slot):
                            mm = pe.matmul(dst, wo_kv[:, :], s[:, part(n, p, at)], start=True, stop=True)
                        mm.then_inc(o_mm, 1)
                if left:
                    for p in range(2):
                        centered("2", free(("c2", p)), b, p, 2 * (t - 1) + p + 1)
                    slot = free(("v2", 0))
                    for p in range(2):
                        pe.wait_ge(sq_ready["2"], 2 * (t - 1) + p + 1)
                        mm = mean_rows(tile[slot][0:ROWS, 0:ROW], slide, ROWS, sq2[:, p, :], p * ROWS_PER_PAIR,
                                       p == 0, p == 1)
                    mm.then_inc(var_mm["2"], 1)
                if attend:
                    for p in range(2):
                        centered("1", free(("c1", p)), n, p, 2 * t + p + 1)
                    for p in range(2):
                        slot = free(("v1", p))
                        pe.wait_ge(sq_ready["1"], 2 * t + p + 1)
                        mean_rows(tile[slot][0:ROWS_PER_PAIR, 0:ROW], slide, ROWS_PER_PAIR, sq1[:, p, :], 0,
                                  True, True).then_inc(var_mm["1"], 1)
                    first_rstd(0)
                    up(0, 0)
                    up(0, 1)
                    first_rstd(1)
                    up(0, 2)
                    up(0, 3)
                    up(1, 0)
                    second_rstd(0)
                    up(1, 1)
                    second_rstd(1)
                    up(1, 2)
                    up(1, 3)
                else:
                    second_rstd(0)
                    second_rstd(1)

            pe.wait_ge(const_ready, 9)
            pe.wait_ge(gam_step, 2)
            for n in range(2):
                mm = pe.matmul(tile[0][:, n:n + 1], ones[:, :], gam[:, n, 0:1], start=True, stop=True)
            mm.then_inc(gam_mm, 1)
            pe.wait_ge(tern_step, 10)
            for j in range(FT):
                mm = pe.matmul(tile[1][:, 0:1], pw[:, j * P:(j + 1) * P], ffn_norm[:, FT + j:FT + j + 1],
                               start=(j == 0), stop=(j == FT - 1))
            mm.then_inc(cb_mm, 1)
            pe.wait_ge(gam_step, 3 + FT)
            for j in range(FT):
                mm = pe.matmul(tile[2][:, 0:P], ones_ff[:, :], pw[:, j * P:(j + 1) * P], start=(j == 0), stop=(j == FT - 1))
            mm.then_inc(pw_mm, 1)
            pe.wait_ge(gam_step, 3 + 2 * FT)

            step(0, 0, 0, left=False)
            with pe.Fori(0, LAYERS - 1) as i:
                step(2 * i + 1, 1, i)
                step(2 * i + 2, 0, i + 1)
            step(STEPS - 1, 1, LAYERS - 1)
            step(STEPS, 0, LAYERS, attend=False)

            def last(key):
                at = LAST.index(key) - RING
                if at >= 0:
                    pe.wait_ge(*last_reader(LAST[at]))
                slot = last_slot_of(key)
                kind, p = key[0], key[1]
                n, q = p // 2, p % 2
                if kind in ("cx", "cz"):
                    centered(kind[1], slot, n, q, p + 1)
                elif kind in ("vx", "vz"):
                    k = kind[1]
                    for q in range(2):
                        pe.wait_ge(sq_ready[k], 2 * p + q + 1)
                        mm = mean_rows(tile[slot][0:ROWS, 0:ROW], slide, ROWS, squares_of[k][:, q, :],
                                       q * ROWS_PER_PAIR, q == 0, q == 1)
                    mm.then_inc(var_mm[k], 1)
                elif kind in ("rx", "rz"):
                    k = kind[1]
                    pe.wait_ge(r_ready[k], 2 * (n + 1))
                    spread(slot, (rr2, rr3)[n][:, :], ROWS, q * ROWS_PER_PAIR).then_inc(r_mm[k], 1)
                elif kind == "h":
                    j = key[2]
                    pe.wait_ge(x_lo["x"], p + 1)
                    for dst, at in halves(slot):
                        c = part(n, q, at)
                        pe.matmul(dst, tfc[:, j * P:(j + 1) * P], xh[:, c], start=True, stop=False)
                        mm = pe.matmul(dst, tfc[:, j * P:(j + 1) * P], xl[:, c], start=False, stop=True)
                    mm.then_inc(h_mm, 1)
                elif kind == "f":
                    pe.wait_ge(h_ready, 2 * FT * STEPS + (p + 1) * FT)
                    for dst, at in halves(slot):
                        for j in range(FT):
                            mm = pe.matmul(dst, pw[:, j * P:(j + 1) * P], h[:, q, j * PAIR + at:j * PAIR + at + BANK],
                                           start=(j == 0), stop=(j == FT - 1))
                    mm.then_inc(f_mm, 1)
                elif kind == "g":
                    pe.wait_ge(g_part, (p + 1) * (FT - 1))
                    pe.wait_ge(s_sum, (p + 1) * (FT - 1))
                    for bank, src in enumerate((kw, a1)):
                        mean_rows(tile[slot][0:ROWS_PER_PAIR, bank * BANK:bank * BANK + ROW], slide_ff, ROWS_PER_PAIR,
                                  src[:, q, :], 0, True, True).then_inc(g_mm, 1)
                elif kind == "rf":
                    pe.wait_ge(r_ready["g"], 2 * (p + 1))
                    spread(slot, rr1[:, q, :], ROWS_PER_PAIR, 0).then_inc(rf_mm, 1)

            for key in LAST:
                last(key)



def kernel(**inputs):
    import numpy as np
    import concourse.bacc as bacc
    from concourse.bass_utils import run_bass_kernel_spmd

    g = {n: np.asarray(v) for n, v in inputs.items()}
    at = lambda n: g["L0_attn_" + n]
    hidden_tiles = lambda w: w.reshape(w.shape[:-2] + (FT, P, w.shape[-1])).swapaxes(-3, -2).reshape(
        w.shape[:-2] + (P, FT * w.shape[-1]))
    vectors = [at(n)[:, :, None] for n in ("bq", "bk", "bv", "bo", "ln1_s", "ln1_b", "b2", "ln2_s", "ln2_b")]
    vectors.append(at("b1").reshape(LAYERS, FT, P).swapaxes(1, 2))
    layers = np.concatenate([at("Wq"), at("Wk"), at("Wv"), at("Wo"), at("W1"), hidden_tiles(at("W2"))] + vectors, axis=2)
    arrays = {
        "x_t": at("x").reshape(TOKENS, P).T,
        "layers": layers,
        "fc_t": g["L0_ffn_W_fc"].T,
        "proj_t": hidden_tiles(g["L0_ffn_W_proj"].T),
        "ffn_ln": np.concatenate([g["L0_ffn_ln_w"].reshape(FT, P).T, g["L0_ffn_ln_b"].reshape(FT, P).T], axis=1),
    }
    arrays = {n: np.ascontiguousarray(v) for n, v in arrays.items()}
    nc = bacc.Bacc("TRN2", target_bir_lowering=False, num_devices=1)
    args = [nc.dram_tensor(n, v.shape, mybir.dt.from_np(v.dtype), kind="ExternalInput").ap() for n, v in arrays.items()]
    out = nc.dram_tensor("out_t", (P, TOKENS), F32, kind="ExternalOutput").ap()
    build(nc, *args, out)
    r = run_bass_kernel_spmd(nc, [arrays], core_ids=[0])
    return np.ascontiguousarray(r.results[0]["out_t"].T).reshape(BATCHES, SEQ, P)
```
